# Optimizing a Trainium2 kernel written in Bass

```python
import numpy as np
import jax
import jax.numpy as jnp

def _softmax(x, axis=-1):
    return jax.nn.softmax(x, axis=axis)

def _gelu(x):
    return jax.nn.gelu(x, approximate=True)

def _silu(x):
    return jax.nn.silu(x)

def _sigmoid(x):
    return jax.nn.sigmoid(x)

def _layernorm(x, axis=-1, eps=1e-05):
    m = jnp.mean(x, axis=axis, keepdims=True)
    v = jnp.var(x, axis=axis, keepdims=True)
    return (x - m) / jnp.sqrt(v + eps)

def _scatter_add(tgt, idx, src, axis=0):
    return tgt.at[idx].add(src)

def _segment_sum(src, seg, n):
    return jax.ops.segment_sum(src, seg, n)
kernel_name = 'mk_prb_d1_jaxref_r4_553093'

def setup_inputs(seed: int=0):
    np.random.seed(seed)
    _w = jnp.asarray

    def _L0_attn_setup():
        import jax, jax.numpy as jnp
        import numpy as np
        B, N, D_IN, D_OUT, H = (2, 512, 256, 256, 16)
        HEAD_DIM = D_OUT // H
        key = jax.random.key(seed)
        ks = jax.random.split(key, 8)
        s = 0.02
        return {'x': jax.random.normal(ks[0], (B, N, D_IN), dtype=jnp.float32), 'Wq': jax.random.normal(ks[1], (D_IN, D_OUT), dtype=jnp.float32) * s, 'Wk': jax.random.normal(ks[2], (D_IN, D_OUT), dtype=jnp.float32) * s, 'Wv': jax.random.normal(ks[3], (D_IN, D_OUT), dtype=jnp.float32) * s, 'Wo': jax.random.normal(ks[4], (D_OUT, D_OUT), dtype=jnp.float32) * s, 'bo': jnp.zeros((D_OUT,), dtype=jnp.float32), 'w': jax.random.uniform(ks[5], (H,), dtype=jnp.float32), 'v': jax.random.uniform(ks[6], (H,), dtype=jnp.float32)}
    _L0_attn_in = _L0_attn_setup()

    def _L0_ffn_setup():
        import jax, jax.numpy as jnp
        import numpy as np
        E = 8
        TOPK = 2
        SCALE = 2.0
        key = jax.random.key(seed)
        ks = jax.random.split(key, 12)
        B, S, D, F, R = (2, 128, 256, 1024, 16)
        w = lambda k, shp: jax.random.normal(k, shp, dtype=jnp.float32) * 0.02
        return {'hidden_states': jax.random.normal(ks[0], (B, S, D), dtype=jnp.float32), 'gate_w': w(ks[1], (E, D)), 'w_gate': w(ks[2], (F, D)), 'w_up': w(ks[3], (F, D)), 'w_down': w(ks[4], (D, F)), 'A1': w(ks[5], (E, R, D)), 'B1': w(ks[6], (E, F, R)), 'A3': w(ks[7], (E, R, D)), 'B3': w(ks[8], (E, F, R)), 'A2': w(ks[9], (E, R, F)), 'B2': w(ks[10], (E, D, R))}
    _L0_ffn_in = _L0_ffn_setup()
    _d = {'L0_attn_x': _L0_attn_in['x'], 'L0_attn_Wq': _L0_attn_in['Wq'], 'L0_attn_Wk': _L0_attn_in['Wk'], 'L0_attn_Wv': _L0_attn_in['Wv'], 'L0_attn_Wo': _L0_attn_in['Wo'], 'L0_attn_bo': _L0_attn_in['bo'], 'L0_attn_w': _L0_attn_in['w'], 'L0_attn_v': _L0_attn_in['v'], 'L0_ffn_gate_w': _L0_ffn_in['gate_w'], 'L0_ffn_w_gate': _L0_ffn_in['w_gate'], 'L0_ffn_w_up': _L0_ffn_in['w_up'], 'L0_ffn_w_down': _L0_ffn_in['w_down'], 'L0_ffn_A1': _L0_ffn_in['A1'], 'L0_ffn_B1': _L0_ffn_in['B1'], 'L0_ffn_A3': _L0_ffn_in['A3'], 'L0_ffn_B3': _L0_ffn_in['B3'], 'L0_ffn_A2': _L0_ffn_in['A2'], 'L0_ffn_B2': _L0_ffn_in['B2']}
    _x0 = _d['L0_attn_x']
    _d['L0_attn_x'] = jax.random.normal(jax.random.fold_in(jax.random.key(seed), 1), (4, 2048, 256), dtype=_x0.dtype)
    del _x0
    return _d

def reference(L0_attn_x, L0_attn_Wq, L0_attn_Wk, L0_attn_Wv, L0_attn_Wo, L0_attn_bo, L0_attn_w, L0_attn_v, L0_ffn_gate_w, L0_ffn_w_gate, L0_ffn_w_up, L0_ffn_w_down, L0_ffn_A1, L0_ffn_B1, L0_ffn_A3, L0_ffn_B3, L0_ffn_A2, L0_ffn_B2):

    def _L0_attn_ref(x, Wq, Wk, Wv, Wo, bo, w, v):
        import jax, jax.numpy as jnp
        import numpy as np
        B, N, D_IN, D_OUT, H = (2, 512, 256, 256, 16)
        HEAD_DIM = D_OUT // H
        b, n, _ = x.shape
        h = w.shape[0]
        hd = Wq.shape[1] // h

        def proj(W):
            return (x @ W).reshape(b, n, h, hd).transpose(0, 2, 1, 3)
        q, k, val = (proj(Wq), proj(Wk), proj(Wv))
        pos = jnp.arange(n)
        R = jnp.abs(pos[:, None] - pos[None, :]).astype(x.dtype)
        wv = w[:, None, None]
        vv = v[:, None, None]
        R_hat = (1.0 + jnp.exp(vv)) / (1.0 + jnp.exp(vv - wv * R))
        scores = jax.nn.relu(jnp.einsum('bhqd,bhkd->bhqk', q, k)) * R_hat[None]
        causal = jnp.triu(jnp.ones((n, n), dtype=bool), k=1)
        scores = jnp.where(causal[None, None], -jnp.inf, scores)
        attn = jax.nn.softmax(scores / np.sqrt(hd).astype(x.dtype), axis=-1)
        ctx = jnp.einsum('bhqk,bhkd->bhqd', attn, val)
        ctx = ctx.transpose(0, 2, 1, 3).reshape(b, n, h * hd)
        return ctx @ Wo + bo

    def _L0_ffn_ref(hidden_states, gate_w, w_gate, w_up, w_down, A1, B1, A3, B3, A2, B2):
        import jax, jax.numpy as jnp
        import numpy as np
        E = 8
        TOPK = 2
        SCALE = 2.0
        B, S, D = hidden_states.shape
        x = hidden_states.reshape(-1, D)
        N = x.shape[0]
        probs = jax.nn.softmax(x @ gate_w.T, axis=-1)
        vals, idx = jax.lax.top_k(probs, TOPK)
        rw = vals / jnp.sum(vals, axis=-1, keepdims=True)
        weight = jnp.zeros((N, E), x.dtype).at[jnp.arange(N)[:, None], idx].add(rw)
        common_w1 = x @ w_gate.T
        common_w3 = x @ w_up.T
        d1 = jnp.einsum('enr,efr->enf', jnp.einsum('nd,erd->enr', x, A1), B1) * SCALE
        d3 = jnp.einsum('enr,efr->enf', jnp.einsum('nd,erd->enr', x, A3), B3) * SCALE
        act = jax.nn.silu(common_w1[None] + d1) * (common_w3[None] + d3)
        out = jnp.einsum('ne,enf->nf', weight, act) @ w_down.T
        z = jnp.einsum('enf,erf->enr', act, A2)
        out = out + jnp.einsum('ne,enr,edr->nd', weight, z, B2) * SCALE
        return out.reshape(B, S, D)
    x = L0_attn_x
    xn = _layernorm(x, axis=-1)
    x = x + _L0_attn_ref(xn, L0_attn_Wq, L0_attn_Wk, L0_attn_Wv, L0_attn_Wo, L0_attn_bo, L0_attn_w, L0_attn_v) + _L0_ffn_ref(xn, L0_ffn_gate_w, L0_ffn_w_gate, L0_ffn_w_up, L0_ffn_w_down, L0_ffn_A1, L0_ffn_B1, L0_ffn_A3, L0_ffn_B3, L0_ffn_A2, L0_ffn_B2)
    return x

_drawn_inputs = setup_inputs


def setup_inputs(seed=0):
    import zlib

    import numpy as np

    out = dict(_drawn_inputs(seed))
    spreads = {'L0_attn_bo': (0.0, 2.0)}
    factors = {'L0_attn_Wq': 8.0,
     'L0_attn_Wk': 8.0,
     'L0_attn_Wv': 8.0,
     'L0_attn_Wo': 8.0,
     'L0_attn_w': 8.0,
     'L0_attn_v': 8.0,
     'L0_ffn_gate_w': 8.0,
     'L0_ffn_A1': 8.0,
     'L0_ffn_B1': 8.0,
     'L0_ffn_A3': 8.0,
     'L0_ffn_B3': 8.0,
     'L0_ffn_A2': 8.0,
     'L0_ffn_B2': 8.0}
    for name, (base, spread) in spreads.items():
        noise = np.random.default_rng([zlib.crc32(name.encode()), seed]).standard_normal(out[name].shape)
        drawn = base * np.exp(spread * noise) if base else spread * noise
        out[name] = jnp.asarray(drawn.astype(out[name].dtype))
    for name, factor in factors.items():
        out[name] = (out[name] * factor).astype(out[name].dtype)
    return out
```

```python
import concourse.bass as bass
from concourse import mybir
from contextlib import ExitStack

F32 = mybir.dt.float32
BF16 = mybir.dt.bfloat16
F16 = mybir.dt.float16
U32 = mybir.dt.uint32
ALU = mybir.AluOpType
ACT = mybir.ActivationFunctionType

P = 128
B, N, D = 4, 2048, 256
H, HD = 16, 16
F, E, R = 1024, 8, 16
ER = E * R
EPS = 1e-5
LORA_SCALE = 2.0
DT = D // P
FT = F // P
G = 512
GT = G // P
GB = N // G
TT = B * N // P
UW = 2 * ER + E
YW = D + ER
NP = 3
QK_STORES = 2 * DT * NP


def ffn_and_projections(nc, x, wq, wk, wv, bo, x_cols, wg, wu, b1, b3, wda, b2, q_parts, k_parts, y_dram, v_all, ident):
    ctx = ExitStack()
    with ctx:
        def sb(name, shape, dt=F32):
            return ctx.enter_context(nc.sbuf_tensor(name, shape, dt))

        def sem(name):
            return ctx.enter_context(nc.semaphore(name))

        wq_sb, wk_sb, wv_sb = (sb(n, [P, DT, D]) for n in ("wq_sb", "wk_sb", "wv_sb"))
        cols_sb = sb("cols_sb", [P, DT, UW])
        wg_sb, wu_sb = sb("wg_sb", [P, DT, F]), sb("wu_sb", [P, DT, F])
        b1_sb, b3_sb = sb("b1_sb", [P, F]), sb("b3_sb", [P, F])
        wda_sb = sb("wda_sb", [P, FT, YW])
        b2_sb = sb("b2_sb", [P, D])
        bo_sb = sb("bo_sb", [P, D])
        expert_of = sb("expert_of", [P, 2 * ER])
        eps_col = sb("eps_col", [P, 1])

        x_sb = sb("x_sb", [P, GT, D])
        bn = sb("bn", [P, GT, 6])
        mean_var = sb("mean_var", [P, GT, 2])
        std = sb("std", [P, GT])
        rstd = sb("rstd", [P, GT])
        xn = sb("xn", [P, GT, D])
        xnT = sb("xnT", [P, DT, G])
        parts = sb("parts", [P, 2 * DT, NP, G], BF16)
        rest = sb("rest", [P, 2, G])
        u_sb = sb("u_sb", [P, GT, UW])
        top = sb("top", [P, GT, 8])
        top_at = sb("top_at", [P, GT, 8], U32)
        chosen = sb("chosen", [P, GT, 2])
        dlogit = sb("dlogit", [P, GT])
        edl = sb("edl", [P, GT])
        den = sb("den", [P, GT])
        rw = sb("rw", [P, 2, GT])
        lora = sb("lora", [P, 2, GT, 2 * ER])
        loraT = sb("loraT", [P, 2, 2, G])
        silu = sb("silu", [P, 3, G])
        act = sb("act", [P, 2, FT, G])
        y_sb = sb("y_sb", [P, GT, D])
        z_a, z_w = lora[:, 0, :, 0:ER], lora[:, 0, :, ER:2 * ER]
        z_b, z_sb = lora[:, 1, :, 0:ER], lora[:, 1, :, ER:2 * ER]
        zT = sb("zT", [P, G])
        ps = ctx.enter_context(nc.psum_tensor("ps", [P, 8, G], F32))

        weights_in, bo_in, ident_in = sem("weights_in"), sem("bo_in"), sem("ident_in")
        consts = sem("consts")
        ident_step = sem("ident_step")
        x_in, y_begun = sem("x_in"), sem("y_begun")
        bn_done, stats_done, std_done, rstd_done, xn_done = (sem(n) for n in ("bn_done", "stats_done", "std_done", "rstd_done", "xn_done"))
        xT_psum, xT_done = sem("xT_psum"), sem("xT_done")
        qk_psum, part1_done, rest_done, part2_done, parts_done = (sem(n) for n in ("qk_psum", "part1_done", "rest_done", "part2_done", "parts_done"))
        qk_stored = sem("qk_stored")
        v_psum, v_done = sem("v_psum"), sem("v_done")
        u_psum, u_done = sem("u_psum"), sem("u_done")
        top_done, at_done, chosen_done, dl_done, edl_done, den_done, rw0_done = (
            sem(n) for n in ("top_done", "at_done", "chosen_done", "dl_done", "edl_done", "den_done", "rw0_done"))
        rw_done = sem("rw_done")
        masked, lora_done = sem("masked"), sem("lora_done")
        loraT_psum, loraT_done = sem("loraT_psum"), sem("loraT_done")
        h_psum, silu_done, act_done = sem("h_psum"), sem("silu_done"), sem("act_done")
        y_psum, y_used = sem("y_psum"), sem("y_used")
        y_step = sem("y_step")
        zm_done, zw_done, z_done = sem("zm_done"), sem("zw_done"), sem("z_done")
        zT_psum, zT_done = sem("zT_psum"), sem("zT_done")
        yl_psum, y_done, y_stored = sem("yl_psum"), sem("y_done"), sem("y_stored")
        scaled = sem("scaled")

        jobs = [(0, 0)]
        for f in range(1, FT):
            jobs += [(f, 0), (f - 1, 1)]
        jobs += [(FT - 1, 1)]
        at = {job: n for n, job in enumerate(jobs)}
        NJ = len(jobs)

        weight_loads = [
            (wq_sb[:], wq.rearrange("(t p) c -> p t c", p=P)), (wk_sb[:], wk.rearrange("(t p) c -> p t c", p=P)),
            (wv_sb[:], wv.rearrange("(t p) c -> p t c", p=P)), (cols_sb[:], x_cols.rearrange("(t p) c -> p t c", p=P)),
            (wg_sb[:], wg.rearrange("(t p) c -> p t c", p=P)), (wu_sb[:], wu.rearrange("(t p) c -> p t c", p=P)),
            (b1_sb[:], b1), (b3_sb[:], b3), (wda_sb[:], wda.rearrange("(t p) c -> p t c", p=P)), (b2_sb[:], b2),
        ]
        block = ctx.enter_context(nc.Block())

        @block.sync
        def _(sp):
            def group(g, b, gb):
                sp.wait_ge(xn_done, g + 1)
                sp.dma_start(x_sb[:], x[bass.ds(b, 1), bass.ds(gb * G, G), :].rearrange("a (t p) d -> p (a t) d", p=P)).then_inc(x_in, 16)

            def stores(g, b, gb):
                for m in range(2 * DT):
                    sp.wait_ge(parts_done, g * (2 * DT) + m + 1)
                    dst = (q_parts if m < DT else k_parts)
                    for a in range(NP):
                        hh = H // DT
                        sp.dma_start(dst[(m % DT) * hh:(m % DT + 1) * hh, bass.ds(b, 1), a, :, bass.ds(gb * G, G)].rearrange("h a d t -> h (a d) t"),
                                     parts[:, m, a, :]).then_inc(qk_stored, 16)
                sp.wait_ge(y_done, g + 1)
                sp.dma_start(y_dram[bass.ds(b, 1), bass.ds(gb * G, G), :].rearrange("a (t p) d -> p (a t) d", p=P), y_sb[:]).then_inc(y_stored, 16)

            sp.dma_start(bo_sb[:], bo.rearrange("(a n) -> a n", a=1).to_broadcast([P, D])).then_inc(bo_in, 16)
            with sp.Fori(0, B) as b:
                with sp.Fori(0, GB) as gb:
                    g = b * GB + gb
                    group(g, b, gb)
                    stores(g, b, gb)
            sp.wait_ge(qk_stored, 16 * QK_STORES * B * GB + 16)
            sp.wait_ge(y_stored, 16 * B * GB + 16)

        @block.gpsimd
        def _(pool):
            nc.gpsimd.memset(ident[:], 0.0).then_inc(ident_step, 1)
            pool.wait_ge(ident_step, 1)
            nc.gpsimd.affine_select(out=ident[:], in_=ident[:], compare_op=ALU.not_equal, fill=1.0, base=0,
                                    pattern=[[-1, P]], channel_multiplier=1).then_inc(consts, 1)
            nc.gpsimd.iota(expert_of[:], pattern=[[0, 2], [1, E], [0, R]], base=0, channel_multiplier=0,
                           allow_small_or_imprecise_dtypes=True).then_inc(consts, 1)
            nc.gpsimd.memset(eps_col[:], EPS).then_inc(consts, 1)
            for free, n in ((xn_done, 1), (y_stored, 16), (qk_stored, 16)):
                pool.sem_inc(free, n)

        @block.scalar
        def _(act_e):
            for dst, src in weight_loads:
                act_e.dma_start(dst, src).then_inc(weights_in, 16)
            act_e.wait_ge(consts, 3)
            with act_e.Fori(0, B * GB) as g:
                act_e.wait_ge(stats_done, g + 1)
                nc.scalar.activation(std[:], mean_var[:, :, 1], ACT.Sqrt, bias=eps_col[:]).then_inc(std_done, 1)
                for t in range(DT):
                    act_e.wait_ge(xT_psum, g * DT + t + 1)
                    nc.scalar.activation(xnT[:, t, :], ps[:, t, :], ACT.Copy).then_inc(xT_done, 1)
                for t in range(2):
                    act_e.wait_ge(v_psum, g * 2 + t + 1)
                    nc.scalar.activation(v_all[:, bass.ds(g * GT + 2 * t, 2), :].rearrange("p t d -> p (t d)"), ps[:, t, :], ACT.Copy).then_inc(v_done, 1)
                for t in range(GT):
                    act_e.wait_ge(u_psum, g * GT + t + 1)
                    nc.scalar.activation(u_sb[:, t, :], ps[:, (6 + t) % 8, 0:UW], ACT.Copy).then_inc(u_done, 1)
                act_e.wait_ge(dl_done, g + 1)
                nc.scalar.activation(edl[:], dlogit[:], ACT.Exp).then_inc(edl_done, 1)
                for n in range(4):
                    act_e.wait_ge(loraT_psum, g * 4 + n + 1)
                    nc.scalar.activation(loraT[:, n // 2, n % 2, :], ps[:, 2 + n, :], ACT.Copy).then_inc(loraT_done, 1)
                for n, (f, s) in enumerate(jobs):
                    act_e.wait_ge(h_psum, g * NJ + n + 1)
                    if n >= 3:
                        act_e.wait_ge(act_done, g * NJ + n - 2)
                    nc.scalar.activation(silu[:, n % 3, :], ps[:, 2 * (f % 3), :], ACT.Silu).then_inc(silu_done, 1)
                act_e.wait_ge(zT_psum, g + 1)
                nc.scalar.activation(zT[:], ps[:, 0, :], ACT.Copy).then_inc(zT_done, 1)

        @block.vector
        def _(dve):
            dve.wait_ge(weights_in, 16 * len(weight_loads))
            for n, w in enumerate((b1_sb, b3_sb, b2_sb)):
                nc.vector.tensor_scalar(w[:], w[:], LORA_SCALE, None, ALU.mult).then_inc(scaled, 1)
            dve.wait_ge(bo_in, 16)
            dve.wait_ge(consts, 3)
            with dve.Fori(0, B * GB) as g:
                dve.wait_ge(x_in, g * 16 + 16)
                for t in range(GT):
                    nc.vector.bn_stats(bn[:, t, :], x_sb[:, t, :]).then_inc(bn_done, 1)
                dve.wait_ge(y_stored, g * 16 + 16)
                dve.wait_ge(bn_done, g * GT + GT)
                nc.vector.tensor_tensor(y_sb[:], x_sb[:], bo_sb[:].unsqueeze(1).to_broadcast([P, GT, D]), ALU.add).then_inc(y_begun, 1)
                for t in range(GT):
                    last = nc.vector.bn_aggr(mean_var[:, t, :], bn[:, t, :])
                last.then_inc(stats_done, 1)
                dve.wait_ge(std_done, g + 1)
                nc.vector.reciprocal(rstd[:], std[:]).then_inc(rstd_done, 1)
                dve.wait_ge(rstd_done, g + 1)
                for t in range(GT):
                    last = nc.vector.tensor_scalar(xn[:, t, :], x_sb[:, t, :], mean_var[:, t, 0:1], rstd[:, t:t + 1], ALU.subtract, ALU.mult)
                last.then_inc(xn_done, 1)
                dve.wait_ge(qk_stored, g * (16 * QK_STORES) + 16)
                for m in range(2 * DT):
                    dve.wait_ge(qk_psum, g * (2 * DT) + m + 1)
                    nc.vector.tensor_copy(parts[:, m, 0, :], ps[:, 2 + m, :]).then_inc(part1_done, 1)
                    dve.wait_ge(part1_done, g * (2 * DT) + m + 1)
                    nc.vector.tensor_tensor(rest[:, m % 2, :], ps[:, 2 + m, :], parts[:, m, 0, :], ALU.subtract).then_inc(rest_done, 1)
                    dve.wait_ge(rest_done, g * (2 * DT) + m + 1)
                    nc.vector.tensor_copy(parts[:, m, 1, :], rest[:, m % 2, :]).then_inc(part2_done, 1)
                    if m == 2 * DT - 1:
                        dve.wait_ge(u_done, g * GT + GT)
                    dve.wait_ge(part2_done, g * (2 * DT) + m + 1)
                    nc.vector.tensor_tensor(parts[:, m, 2, :], rest[:, m % 2, :], parts[:, m, 1, :], ALU.subtract).then_inc(parts_done, 1)
                for t in range(GT):
                    nc.vector.max(top[:, t, :], u_sb[:, t, 2 * ER:UW]).then_inc(top_done, 1)
                dve.wait_ge(top_done, g * GT + GT)
                nc.vector.tensor_tensor(dlogit[:], top[:, :, 1], top[:, :, 0], ALU.subtract).then_inc(dl_done, 1)
                for t in range(GT):
                    last = nc.vector.max_index(top_at[:, t, :], top[:, t, :], u_sb[:, t, 2 * ER:UW])
                last.then_inc(at_done, 1)
                dve.wait_ge(at_done, g + 1)
                nc.vector.tensor_copy(chosen[:], top_at[:, :, 0:2]).then_inc(chosen_done, 1)
                dve.wait_ge(chosen_done, g + 1)
                for s in range(2):
                    for t in range(GT):
                        last = nc.vector.scalar_tensor_tensor(out=lora[:, s, t, :], in0=expert_of[:], scalar=chosen[:, t, s:s + 1],
                                                              in1=u_sb[:, t, 0:2 * ER], op0=ALU.is_equal, op1=ALU.mult)
                last.then_inc(masked, 1)
                dve.wait_ge(masked, g + 1)
                nc.vector.tensor_tensor(lora[:, 1, :, :], lora[:, 1, :, :], lora[:, 0, :, :], ALU.subtract).then_inc(lora_done, 1)
                dve.wait_ge(edl_done, g + 1)
                nc.vector.tensor_scalar(den[:], edl[:], 1.0, None, ALU.add).then_inc(den_done, 1)
                dve.wait_ge(den_done, g + 1)
                nc.vector.reciprocal(rw[:, 0, :], den[:]).then_inc(rw0_done, 1)
                dve.wait_ge(rw0_done, g + 1)
                nc.vector.tensor_tensor(rw[:, 1, :], edl[:], rw[:, 0, :], ALU.mult).then_inc(rw_done, 1)
                dve.wait_ge(rw_done, g + 1)
                for n, (f, s) in enumerate(jobs):
                    dve.wait_ge(silu_done, g * NJ + n + 1)
                    nc.vector.tensor_tensor(act[:, s, f, :], ps[:, 2 * (f % 3) + 1, :], silu[:, n % 3, :], ALU.mult).then_inc(act_done, 1)
                for t in range(GT):
                    for s in range(2):
                        k = t * 2 + s
                        dve.wait_ge(y_psum, g * (2 * GT) + k + 1)
                        if k == 0:
                            dve.wait_ge(y_begun, g + 1)
                        if s:
                            dve.wait_ge(y_step, g * (2 * GT) + k)
                        nc.vector.scalar_tensor_tensor(out=y_sb[:, t, :], in0=ps[:, 6 + s, 0:D], scalar=rw[:, s, t:t + 1],
                                                       in1=y_sb[:, t, :], op0=ALU.mult, op1=ALU.add).then_inc(y_step, 1)
                        nc.vector.scalar_tensor_tensor(out=(z_b if s else z_a)[:, t, :], in0=expert_of[:, 0:ER], scalar=chosen[:, t, s:s + 1],
                                                       in1=ps[:, 6 + s, D:YW], op0=ALU.is_equal, op1=ALU.mult).then_inc(y_used, 1)
                for t in range(GT):
                    dve.wait_ge(y_used, g * (2 * GT) + 2 * t + 1)
                    nc.vector.tensor_scalar(z_w[:, t, :], z_a[:, t, :], rw[:, 0, t:t + 1], None, ALU.mult).then_inc(zw_done, 1)
                for t in range(GT):
                    dve.wait_ge(y_used, g * (2 * GT) + 2 * t + 2)
                    dve.wait_ge(zw_done, g * GT + t + 1)
                    last = nc.vector.scalar_tensor_tensor(out=z_sb[:, t, :], in0=z_b[:, t, :], scalar=rw[:, 1, t:t + 1],
                                                          in1=z_w[:, t, :], op0=ALU.mult, op1=ALU.add)
                last.then_inc(z_done, 1)
                dve.wait_ge(yl_psum, g + 1)
                dve.wait_ge(y_step, g * (2 * GT) + 2 * GT)
                nc.vector.tensor_tensor(y_sb[:].rearrange("p t d -> p (t d)"), ps[:, 2:4, :].rearrange("p t d -> p (t d)"), y_sb[:].rearrange("p t d -> p (t d)"), ALU.add).then_inc(y_done, 1)

        @block.tensor
        def _(pe):
            mm = nc.tensor.matmul
            pe.wait_ge(weights_in, 16 * len(weight_loads))
            pe.wait_ge(scaled, 3)
            pe.wait_ge(consts, 3)
            with pe.Fori(0, B * GB) as g:
                pe.wait_ge(xn_done, g + 2)
                for t in range(DT):
                    for i in range(GT):
                        last = nc.tensor.transpose(ps[:, t, i * P:(i + 1) * P], xn[:, i, t * P:(t + 1) * P], ident[:])
                    last.then_inc(xT_psum, 1)
                pe.wait_ge(xT_done, g * DT + DT)
                for m in range(2 * DT):
                    w = wq_sb if m < DT else wk_sb
                    for t in range(DT):
                        last = mm(ps[:, 2 + m, :], w[:, t, (m % DT) * P:(m % DT + 1) * P], xnT[:, t, :], start=(t == 0), stop=(t == DT - 1))
                    last.then_inc(qk_psum, 1)
                for i in range(GT):
                    for t in range(DT):
                        last = mm(ps[:, i // 2, (i % 2) * D:(i % 2 + 1) * D], xnT[:, t, i * P:(i + 1) * P], wv_sb[:, t, :], start=(t == 0), stop=(t == DT - 1))
                    if i % 2:
                        last.then_inc(v_psum, 1)
                for i in range(GT):
                    if i >= 2:
                        pe.wait_ge(v_done, g * 2 + i - 1)
                    for t in range(DT):
                        last = mm(ps[:, (6 + i) % 8, 0:UW], xnT[:, t, i * P:(i + 1) * P], cols_sb[:, t, :], start=(t == 0), stop=(t == DT - 1))
                    last.then_inc(u_psum, 1)
                pe.wait_ge(lora_done, g + 1)
                pe.wait_ge(parts_done, g * (2 * DT) + 2 * DT)
                for s in range(2):
                    for a in range(2):
                        for i in range(GT):
                            last = nc.tensor.transpose(ps[:, 2 + 2 * s + a, i * P:(i + 1) * P], lora[:, s, i, a * ER:(a + 1) * ER], ident[:])
                        last.then_inc(loraT_psum, 1)
                pe.wait_ge(u_done, g * GT + GT)
                pe.wait_ge(loraT_done, g * 4 + 4)
                for n, (f, s) in enumerate(jobs):
                    gate, up = ps[:, 2 * (f % 3), :], ps[:, 2 * (f % 3) + 1, :]
                    cols = slice(f * P, (f + 1) * P)
                    if s == 0:
                        if f >= 3:
                            pe.wait_ge(act_done, g * NJ + at[f - 3, 1] + 1)
                        for t in range(DT):
                            mm(gate, wg_sb[:, t, cols], xnT[:, t, :], start=(t == 0), stop=False)
                        mm(gate, b1_sb[:, cols], loraT[:, 0, 0, :], start=False, stop=True)
                        for t in range(DT):
                            mm(up, wu_sb[:, t, cols], xnT[:, t, :], start=(t == 0), stop=False)
                        last = mm(up, b3_sb[:, cols], loraT[:, 0, 1, :], start=False, stop=True)
                    else:
                        pe.wait_ge(act_done, g * NJ + at[f, 0] + 1)
                        mm(gate, b1_sb[:, cols], loraT[:, 1, 0, :], start=False, stop=True, skip_group_check=True)
                        last = mm(up, b3_sb[:, cols], loraT[:, 1, 1, :], start=False, stop=True, skip_group_check=True)
                    last.then_inc(h_psum, 1)
                for i in range(GT):
                    for s in range(2):
                        k = i * 2 + s
                        if k == 0:
                            pe.wait_ge(act_done, g * NJ + at[FT - 1, 0] + 1)
                        elif k == 1:
                            pe.wait_ge(act_done, g * NJ + NJ)
                        else:
                            pe.wait_ge(y_used, g * (2 * GT) + k - 1)
                        for f in range(FT):
                            last = mm(ps[:, 6 + s, 0:YW], act[:, s, f, i * P:(i + 1) * P], wda_sb[:, f, :], start=(f == 0), stop=(f == FT - 1))
                        last.then_inc(y_psum, 1)
                pe.wait_ge(z_done, g + 1)
                for i in range(GT):
                    last = nc.tensor.transpose(ps[:, 0, i * P:(i + 1) * P], z_sb[:, i, :], ident[:])
                last.then_inc(zT_psum, 1)
                pe.wait_ge(zT_done, g + 1)
                for i in range(GT):
                    last = mm(ps[:, 2 + i // 2, (i % 2) * D:(i % 2 + 1) * D], zT[:, i * P:(i + 1) * P], b2_sb[:], start=True, stop=True)
                last.then_inc(yl_psum, 1)
                pe.wait_ge(y_done, g + 1)


BATCHES_OF_BODY = 2
QT = N // P
SLOT = 1024
CHUNK = 512
CB = CHUNK // P
QW = 32
ROWS = 8 * HD
MASKED = -1e30
SM_SCALE = 1.0 / HD ** 0.5
OG = G // P


def attention(nc, q_parts, k_parts, w, v, v_all, ident, ctx_all):
    ctx = ExitStack()
    with ctx:
        def sb(name, shape, dt=F32):
            return ctx.enter_context(nc.sbuf_tensor(name, shape, dt))

        def sem(name):
            return ctx.enter_context(nc.semaphore(name))

        dist = sb("dist", [P, N], F16)
        factor = sb("factor", [P, N])
        past = sb("past", [P, P])
        hide = sb("hide", [P, P])
        w_neg, v_bc, ev1 = sb("w_neg", [P, H]), sb("v_bc", [P, H]), sb("ev1", [P, H])
        qx = [sb(f"qx{j}", [P, N], BF16) for j in range(BATCHES_OF_BODY)]
        kx = [sb(f"kx{j}", [P, N], BF16) for j in range(BATCHES_OF_BODY)]
        vx = [sb(f"vx{j}", [P, QT, QW]) for j in range(BATCHES_OF_BODY)]
        none = sb("none", [P, QW], BF16)
        rows = [sb(f"rows{i}", [P, N]) for i in range(4)]
        top = sb("row_max", [P, 8])
        unused = sb("unused", [P, 1])
        probs = [sb(f"probs{i}", [P, CHUNK]) for i in range(4)]
        o_parts = [sb(f"o_parts{i}", [P, G]) for i in range(2)]
        fold = sb("fold", [P, QW])
        inv = sb("inv", [P, 2, OG])
        ps = ctx.enter_context(nc.psum_tensor("ps_attn", [P, 8, G], F32))

        const_step, consts, wv_in, wv_done, ev_done = (sem(n) for n in ("const_step", "a_consts", "wv_in", "wv_done", "ev_done"))
        decay_done, factor_step, factor_done = sem("decay_done"), sem("factor_step"), sem("factor_done")
        qk_in = [sem(f"qk_in{j}") for j in range(BATCHES_OF_BODY)]
        vx_done = sem("vx_done")
        s_psum, scaled = sem("s_psum"), sem("s_scaled")
        row_done, diag_done = sem("row_done"), sem("diag_done")
        t_psum, probs_done = sem("t_psum"), sem("probs_done")
        pv_done = sem("pv_done")
        o_done, f_psum = sem("o_done"), sem("f_psum")
        inv_done, normed = sem("inv_done"), sem("normed")

        tiles = [(j, t) for j in range(BATCHES_OF_BODY) for t in range(QT)]
        slots, chunks = [], []
        for n, (j, t) in enumerate(tiles):
            keys = (t + 1) * P
            slots += [(n, k, min(SLOT, keys - k)) for k in range(0, keys, SLOT)]
            chunks += [(n, kb, min(CB, t + 1 - kb)) for kb in range(0, t + 1, CB)]
        NT, NS, NC, NG = len(tiles), len(slots), len(chunks), len(tiles) // OG
        assert NS % 2 == 0 and NC % 4 == 0 and NT % 2 == 0 and NG % 2 == 0
        slots_of = [[c for c, s in enumerate(slots) if s[0] == n] for n in range(NT)]
        chunks_of = [[c for c, s in enumerate(chunks) if s[0] == n] for n in range(NT)]
        last_chunk = [chunks_of[n][-1] for n in range(NT)]
        parts, parts_of = [], []
        for n, (j, t) in enumerate(tiles):
            ends = [(t + 1) * P]
            if n + 1 < NT and len(slots_of[n + 1]) == 2 and t >= CB:
                ends.insert(0, (len(chunks_of[n]) + 1) // 2 * CHUNK)
            parts_of.append(list(range(len(parts), len(parts) + len(ends))))
            parts += [(n, k0, k1) for k0, k1 in zip([0] + ends, ends)]
        NR = len(parts)
        LAG_O, LAG_F = 2, 4
        evac_after = {min(last_chunk[OG * g + OG - 1] + LAG_O, NC - 1): g for g in range(NG)}
        fold_after = {min(last_chunk[OG * g + OG - 1] + LAG_F, NC - 1): g for g in range(NG)}
        LOADS = 5
        BODIES = B // BATCHES_OF_BODY
        credits = [(s_psum, NS), (scaled, 2), (t_psum, NC), (probs_done, 2), (pv_done, NC), (f_psum, 2), (normed, 2)]
        assert len(probs) == 4

        block = ctx.enter_context(nc.Block())

        @block.sync
        def _(sp):
            sp.dma_start(w_neg[:], w.rearrange("(a n) -> a n", a=1).to_broadcast([P, H])).then_inc(wv_in, 16)
            sp.dma_start(v_bc[:], v.rearrange("(a n) -> a n", a=1).to_broadcast([P, H])).then_inc(wv_in, 16)
            with sp.Fori(0, H) as h:
                with sp.Fori(0, BODIES) as bb:
                    for j in range(BATCHES_OF_BODY):
                        b = bb * BATCHES_OF_BODY + j
                        q = q_parts[bass.ds(h, 1), bass.ds(b, 1)].rearrange("h b a d t -> (h b a d) t")
                        k = k_parts[bass.ds(h, 1), bass.ds(b, 1)].rearrange("h b a d t -> (h b a) d t")
                        sp.wait_ge(s_psum, (h * BODIES + bb) * NS + slots_of[(j + 1) * QT - 1][-1] + 1)
                        sp.dma_start(qx[j][0:2 * NP * HD, :], q.unsqueeze(0).to_broadcast([2, NP * HD, N])).then_inc(qk_in[j], 16)
                        sp.dma_start(qx[j][2 * NP * HD:ROWS, :], q[0:2 * HD, :]).then_inc(qk_in[j], 16)
                        for a, (r0, r1) in enumerate(((0, 3), (3, 6), (6, 8))):
                            sp.dma_start(kx[j][r0 * HD:r1 * HD, :], k[a:a + 1].to_broadcast([r1 - r0, HD, N])).then_inc(qk_in[j], 16)

        @block.gpsimd
        def _(pool):
            nc.gpsimd.iota(dist[:], pattern=[[-1, N]], base=N - P, channel_multiplier=1, allow_small_or_imprecise_dtypes=True).then_inc(consts, 1)
            nc.gpsimd.memset(past[:], 1.0).then_inc(const_step, 1)
            nc.gpsimd.memset(hide[:], 0.0).then_inc(const_step, 1)
            nc.gpsimd.memset(fold[:], 0.0).then_inc(const_step, 1)
            nc.gpsimd.memset(none[:], 0.0).then_inc(consts, 1)
            for j in range(BATCHES_OF_BODY):
                nc.gpsimd.memset(vx[j][:], 0.0).then_inc(const_step, 1)
            pool.wait_ge(const_step, 5)
            for j in range(BATCHES_OF_BODY):
                nc.gpsimd.memset(vx[j][:, :, HD:HD + 1], 1.0).then_inc(consts, 1)
            for m, fill in ((past, 0.0), (hide, MASKED)):
                nc.gpsimd.affine_select(out=m[:], in_=m[:], compare_op=ALU.is_ge, fill=fill, base=0,
                                        pattern=[[-1, P]], channel_multiplier=1).then_inc(consts, 1)
            for i in range(CB):
                nc.gpsimd.affine_select(out=fold[:], in_=fold[:], compare_op=ALU.not_equal, fill=1.0, base=-QW * i,
                                        pattern=[[-1, QW]], channel_multiplier=1).then_inc(const_step, 1)
                pool.wait_ge(const_step, 6 + i)
            for free, n in credits:
                pool.sem_inc(free, n)
            pool.wait_ge(consts, 6)
            pool.sem_inc(consts, 1)
            with pool.Fori(0, H) as h:
                with pool.Fori(0, BODIES) as bb:
                    it = h * BODIES + bb
                    for n, (j, t) in enumerate(tiles):
                        if t == 0:
                            pool.wait_ge(pv_done, it * NC + last_chunk[(j + 1) * QT - 1] + 1)
                        pool.wait_ge(row_done, it * NR + parts_of[n][-1] + 1)
                        diag = rows[n % 4][:, t * P:(t + 1) * P]
                        nc.gpsimd.tensor_tensor(diag, diag, hide[:], ALU.add).then_inc(diag_done, 1)
                        if t == 0:
                            nc.gpsimd.tensor_copy(vx[j][:, :, 0:HD], v_all[:, bass.ds((bb * BATCHES_OF_BODY + j) * QT, QT), bass.ds(h * HD, HD)]).then_inc(vx_done, 1)

        @block.scalar
        def _(act_e):
            act_e.wait_ge(wv_in, 32)
            nc.scalar.activation(ev1[:], v_bc[:], ACT.Exp).then_inc(ev_done, 1)
            act_e.wait_ge(wv_done, 3)
            act_e.wait_ge(consts, 7)
            with act_e.Fori(0, H) as h:
                nc.scalar.activation(factor[:], dist[:], ACT.Exp, scale=w_neg[:, bass.ds(h, 1)], bias=v_bc[:, bass.ds(h, 1)]).then_inc(decay_done, 1)
                with act_e.Fori(0, BODIES) as bb:
                    it = h * BODIES + bb
                    for c, (n, kb, m) in enumerate(chunks):
                        act_e.wait_ge(pv_done, it * NC + NC + c - 3)
                        act_e.wait_ge(t_psum, it * NC + NC + c + 1)
                        nc.scalar.activation(probs[c % 4][:, 0:m * P], ps[:, 4 + c % 2, 0:m * P], ACT.Exp, scale=SM_SCALE).then_inc(probs_done, 1)
                        if c in evac_after:
                            g = evac_after[c]
                            act_e.wait_ge(f_psum, it * NG + g + 1)
                            act_e.wait_ge(pv_done, it * NC + NC + last_chunk[OG * g + OG - 1] + 1)
                            nc.scalar.activation(o_parts[g % 2][:], ps[:, 6 + g % 2, :], ACT.Copy).then_inc(o_done, 1)

        @block.vector
        def _(dve):
            dve.wait_ge(wv_in, 32)
            nc.vector.tensor_scalar(w_neg[:], w_neg[:], -1.0, None, ALU.mult).then_inc(wv_done, 1)
            dve.wait_ge(ev_done, 1)
            nc.vector.tensor_scalar(ev1[:], ev1[:], 1.0, None, ALU.add).then_inc(wv_done, 1)
            dve.wait_ge(consts, 7)
            nc.vector.tensor_scalar(dist[:], dist[:], 0.0, None, ALU.max).then_inc(wv_done, 1)
            dve.wait_ge(wv_done, 3)
            with dve.Fori(0, H) as h:
                dve.wait_ge(decay_done, h + 1)
                nc.vector.tensor_scalar(factor[:], factor[:], 1.0, None, ALU.add).then_inc(factor_step, 1)
                dve.wait_ge(factor_step, h * 3 + 1)
                nc.vector.reciprocal(factor[:], factor[:]).then_inc(factor_step, 1)
                dve.wait_ge(factor_step, h * 3 + 2)
                nc.vector.tensor_scalar(factor[:], factor[:], ev1[:, bass.ds(h, 1)], None, ALU.mult).then_inc(factor_step, 1)
                dve.wait_ge(factor_step, h * 3 + 3)
                nc.vector.tensor_tensor(factor[:, N - P:N], factor[:, N - P:N], past[:], ALU.mult).then_inc(factor_done, 1)
                with dve.Fori(0, BODIES) as bb:
                    it = h * BODIES + bb

                    def normalise(g):
                        j, tg = (OG * g) // QT, (OG * g) % QT
                        o = ps[:, 6 + g % 2, 0:OG * QW].rearrange("p (t c) -> p t c", c=QW)
                        dve.wait_ge(f_psum, it * NG + g + 3)
                        nc.vector.reciprocal(inv[:, g % 2, :], o[:, :, HD]).then_inc(inv_done, 1)
                        dve.wait_ge(inv_done, it * NG + g + 1)
                        nc.vector.tensor_tensor(ctx_all[:, bass.ds((bb * BATCHES_OF_BODY + j) * QT + tg, OG), bass.ds(h * HD, HD)], o[:, :, 0:HD],
                                                inv[:, g % 2, :].unsqueeze(2).to_broadcast([P, OG, HD]), ALU.mult).then_inc(normed, 1)

                    norm_at = {}
                    for c, g in fold_after.items():
                        norm_at.setdefault(min(chunks[min(c + 1, NC - 1)][0] + 2, NT), []).append(g)

                    def scale(c):
                        n, k0, kn = slots[c]
                        col = N - P - tiles[n][1] * P + k0
                        so_far = top[:, (c - 1) % 8:(c - 1) % 8 + 1] if k0 else 0.0
                        nc.vector.tensor_tensor_reduce(out=rows[n % 4][:, k0:k0 + kn], in0=ps[:, 2 * (c % 2):2 * (c % 2) + 2, :].rearrange("p a b -> p (a b)")[:, 0:kn],
                                                       in1=factor[:, col:col + kn], scale=1.0, scalar=so_far,
                                                       op0=ALU.mult, op1=ALU.max, accum_out=top[:, c % 8:c % 8 + 1]).then_inc(scaled, 1)

                    def less_max(r):
                        n, k0, k1 = parts[r]
                        c = slots_of[n][-1]
                        nc.vector.tensor_scalar(rows[n % 4][:, k0:k1], rows[n % 4][:, k0:k1], 0.0, top[:, c % 8:c % 8 + 1], ALU.max, ALU.subtract).then_inc(row_done, 1)

                    for n in range(NT):
                        for g in norm_at.get(n, []):
                            normalise(g)
                        c = slots_of[n][0]
                        dve.wait_ge(s_psum, it * NS + NS + c + 1)
                        dve.wait_ge(t_psum, it * NC + (NC + last_chunk[n - 4] if n >= 4 else last_chunk[n + NT - 4]) + 1)
                        if n == 0:
                            dve.wait_ge(factor_done, h + 1)
                            nc.vector.memset(unused[:], 0.0)
                        else:
                            dve.wait_ge(scaled, it * NS + c + 2)
                            for r in parts_of[n - 1][:1 if len(slots_of[n]) == 2 else 2]:
                                less_max(r)
                        scale(c)
                        if len(slots_of[n]) == 2:
                            dve.wait_ge(s_psum, it * NS + NS + c + 2)
                            dve.wait_ge(scaled, it * NS + c + 3)
                            less_max(parts_of[n - 1][1])
                            scale(c + 1)
                    dve.wait_ge(scaled, it * NS + NS + 2)
                    less_max(parts_of[NT - 1][0])
                    for g in norm_at.get(NT, []):
                        normalise(g)

        @block.tensor
        def _(pe):
            mm = nc.tensor.matmul
            pe.wait_ge(consts, 7)
            with pe.Fori(0, H * BODIES) as it:
                def scores(c):
                    n, k0, kn = slots[c]
                    j, t = tiles[n]
                    if t == 0:
                        pe.wait_ge(qk_in[j], it * (16 * LOADS) + 16 * LOADS)
                    pe.wait_ge(scaled, it * NS + c + 1)
                    for i, k in enumerate(range(0, kn, G)):
                        wd = min(G, kn - k)
                        last = mm(ps[:, 2 * (c % 2) + i, 0:wd], qx[j][:, t * P:(t + 1) * P], kx[j][:, k0 + k:k0 + k + wd], start=True, stop=True)
                    last.then_inc(s_psum, 1)

                def transposed(c):
                    n, kb, m = chunks[c]
                    pe.wait_ge(row_done, it * NR + next(r for r in parts_of[n] if parts[r][2] > kb * P) + 1)
                    if c == last_chunk[n]:
                        pe.wait_ge(diag_done, it * NT + n + 1)
                    pe.wait_ge(probs_done, it * NC + c + 1)
                    for i in range(m):
                        last = nc.tensor.transpose(ps[:, 4 + c % 2, i * P:(i + 1) * P], rows[n % 4][:, (kb + i) * P:(kb + i + 1) * P], ident[:])
                    last.then_inc(t_psum, 1)

                def output(c):
                    n, kb, m = chunks[c]
                    j, t = tiles[n]
                    g = n // OG
                    if kb == 0 and t == 0:
                        pe.wait_ge(vx_done, it * BATCHES_OF_BODY + j + 1)
                    if kb == 0 and n % OG == 0:
                        pe.wait_ge(normed, it * NG + g + 1)
                    pe.wait_ge(probs_done, it * NC + c + 3)
                    cols = slice((n % OG) * P, (n % OG + 1) * P)
                    for i in range(CB):
                        o = ps[i * QW:(i + 1) * QW, 6 + g % 2, cols]
                        if i < m:
                            last = mm(o, vx[j][:, kb + i, :], probs[c % 4][:, i * P:(i + 1) * P], start=(kb == 0), stop=(kb + i + CB > t))
                        elif kb == 0:
                            last = mm(o, none[:], kx[j][:, 0:P], start=True, stop=True)
                    last.then_inc(pv_done, 1)

                def folded(g):
                    pe.wait_ge(o_done, it * NG + g + 1)
                    for i in range(OG):
                        last = mm(ps[:, 6 + g % 2, i * QW:(i + 1) * QW], o_parts[g % 2][:, i * P:(i + 1) * P], fold[:], start=True, stop=True)
                    last.then_inc(f_psum, 1)

                for c in slots_of[0] + slots_of[1]:
                    scores(c)
                for n in range(NT):
                    ahead = list(slots_of[n + 2]) if n + 2 < NT else []
                    for c in chunks_of[n]:
                        transposed(c)
                        if ahead:
                            scores(ahead.pop(0))
                        if c:
                            output(c - 1)
                            if c - 1 in fold_after:
                                folded(fold_after[c - 1])
                    for c in ahead:
                        scores(c)
                output(NC - 1)
                folded(fold_after[NC - 1])


def output_projection(nc, wo, y_dram, ctx_all, ident, out):
    ctx = ExitStack()
    with ctx:
        def sb(name, shape, dt=F32):
            return ctx.enter_context(nc.sbuf_tensor(name, shape, dt))

        def sem(name):
            return ctx.enter_context(nc.semaphore(name))

        wo_sb = sb("wo_sb", [P, DT, D])
        y = [sb(f"y{i}", [P, GT, D]) for i in range(2)]
        ctxT = [sb(f"ctxT{i}", [P, DT, G]) for i in range(2)]
        ps = ctx.enter_context(nc.psum_tensor("ps_out", [P, 8, G], F32))
        wo_in, copied = sem("wo_in"), sem("copied")
        y_in = [sem(f"y_in{i}") for i in range(2)]
        stored = [sem(f"stored{i}") for i in range(2)]
        cT_psum, cT_done, a_psum, summed = sem("cT_psum"), sem("cT_done"), sem("a_psum"), sem("summed")
        NGR = B * GB
        y_rows = y_dram.rearrange("b (g t p) d -> (b g) p t d", p=P, t=GT)
        out_rows = out.rearrange("b (g t p) d -> (b g) p t d", p=P, t=GT)
        block = ctx.enter_context(nc.Block())

        @block.sync
        def _(sp):
            sp.dma_start(wo_sb[:], wo.rearrange("(t p) c -> p t c", p=P)).then_inc(wo_in, 16)
            for g in range(2):
                sp.dma_start(y[g][:], y_rows[g]).then_inc(y_in[g], 16)
            for g in range(NGR):
                sp.wait_ge(summed, g + 1)
                sp.dma_start(out_rows[g], y[g % 2][:]).then_inc(stored[g % 2], 16)
                if g + 2 < NGR:
                    sp.wait_ge(stored[g % 2], 16 * (g // 2 + 1))
                    sp.dma_start(y[g % 2][:], y_rows[g + 2]).then_inc(y_in[g % 2], 16)
            for i in range(2):
                sp.wait_ge(stored[i], 16 * (NGR // 2))

        @block.scalar
        def _(act_e):
            for g in range(NGR):
                if g >= 2:
                    act_e.wait_ge(a_psum, g - 1)
                for t in range(DT):
                    act_e.wait_ge(cT_psum, g * DT + t + 1)
                    nc.scalar.activation(ctxT[g % 2][:, t, :], ps[:, 2 * (g % 2) + t, :], ACT.Copy).then_inc(cT_done, 1)

        @block.vector
        def _(dve):
            for g in range(NGR):
                dve.wait_ge(y_in[g % 2], 16 * (g // 2 + 1))
                dve.wait_ge(a_psum, g + 1)
                y2 = y[g % 2][:].rearrange("p t d -> p (t d)")
                nc.vector.tensor_tensor(y2, ps[:, 4 + 2 * (g % 2):6 + 2 * (g % 2), :].rearrange("p t d -> p (t d)"), y2, ALU.add).then_inc(summed, 1)

        @block.tensor
        def _(pe):
            pe.wait_ge(wo_in, 16)

            def transposes(g):
                if g >= 2:
                    pe.wait_ge(cT_done, (g - 1) * DT)
                for t in range(DT):
                    for i in range(GT):
                        last = nc.tensor.transpose(ps[:, 2 * (g % 2) + t, i * P:(i + 1) * P], ctx_all[:, g * GT + i, t * P:(t + 1) * P], ident[:])
                    last.then_inc(cT_psum, 1)

            transposes(0)
            for g in range(NGR):
                if g + 1 < NGR:
                    transposes(g + 1)
                pe.wait_ge(cT_done, (g + 1) * DT)
                if g >= 2:
                    pe.wait_ge(summed, g - 1)
                for i in range(GT):
                    for t in range(DT):
                        last = nc.tensor.matmul(ps[:, 4 + 2 * (g % 2) + i // 2, (i % 2) * D:(i % 2 + 1) * D], ctxT[g % 2][:, t, i * P:(i + 1) * P], wo_sb[:, t, :],
                                                start=(t == 0), stop=(t == DT - 1))
                last.then_inc(a_psum, 1)


def program(nc, x, wq, wk, wv, wo, bo, w, v, x_cols, wg, wu, b1, b3, wda, b2, out):
    ctx = ExitStack()
    with ctx:
        q_parts = nc.dram_tensor("q_parts", [H, B, NP, HD, N], BF16, kind="Internal").ap()
        k_parts = nc.dram_tensor("k_parts", [H, B, NP, HD, N], BF16, kind="Internal").ap()
        y_dram = nc.dram_tensor("y_dram", [B, N, D], F32, kind="Internal").ap()
        v_all = ctx.enter_context(nc.sbuf_tensor("v_all", [P, TT, D], F32))
        ident = ctx.enter_context(nc.sbuf_tensor("ident", [P, P], F32))
        ffn_and_projections(nc, x, wq, wk, wv, bo, x_cols, wg, wu, b1, b3, wda, b2, q_parts, k_parts, y_dram, v_all, ident)
        ctx_all = ctx.enter_context(nc.sbuf_tensor("ctx_all", [P, TT, D], F32))
        attention(nc, q_parts, k_parts, w, v, v_all, ident, ctx_all)
        output_projection(nc, wo, y_dram, ctx_all, ident, out)


def kernel(**inputs):
    import numpy as np
    import concourse.bacc as bacc
    from concourse.bass_utils import run_bass_kernel_spmd

    a = {n.replace("L0_", ""): np.asarray(t) for n, t in inputs.items()}
    flat = lambda t: t.transpose(2, 0, 1).reshape(t.shape[2], -1)
    er = lambda t: t.transpose(0, 2, 1).reshape(ER, -1)
    arrays = {
        "x": a["attn_x"], "wq": a["attn_Wq"], "wk": a["attn_Wk"], "wv": a["attn_Wv"], "wo": a["attn_Wo"], "bo": a["attn_bo"],
        "w": a["attn_w"], "v": a["attn_v"],
        "x_cols": np.concatenate([flat(a["ffn_A1"]), flat(a["ffn_A3"]), a["ffn_gate_w"].T], axis=1),
        "wg": a["ffn_w_gate"].T, "wu": a["ffn_w_up"].T, "b1": er(a["ffn_B1"]), "b3": er(a["ffn_B3"]),
        "wda": np.concatenate([a["ffn_w_down"].T, flat(a["ffn_A2"])], axis=1), "b2": er(a["ffn_B2"]),
    }
    arrays = {n: np.ascontiguousarray(t) for n, t in arrays.items()}
    nc = bacc.Bacc("TRN2", target_bir_lowering=False, num_devices=1)
    args = {n: nc.dram_tensor(n, t.shape, F32, kind="ExternalInput").ap() for n, t in arrays.items()}
    out = nc.dram_tensor("out", [B, N, D], F32, kind="ExternalOutput").ap()
    program(nc, out=out, **args)
    return run_bass_kernel_spmd(nc, [arrays], core_ids=[0]).results[0]["out"]
```

```python
import concourse.bass as bass
from concourse import mybir
from contextlib import ExitStack

F32 = mybir.dt.float32
BF16 = mybir.dt.bfloat16
F16 = mybir.dt.float16
U32 = mybir.dt.uint32
ALU = mybir.AluOpType
ACT = mybir.ActivationFunctionType

P = 128
B, N, D = 4, 2048, 256
H, HD = 16, 16
F, E, R = 1024, 8, 16
ER = E * R
EPS = 1e-5
LORA_SCALE = 2.0
DT = D // P
FT = F // P
G = 512
GT = G // P
GB = N // G
TT = B * N // P
UW = 2 * ER + E
NP = 3
QK_STORES = 2 * DT * NP


PIECES = ["xT0", "xT1", "logits", "u0", "u1", "q0", "q1", "mask0", "mask1", "weight0", "weight1", "k0", "k1", "v0", "v1"]
NPC = len(PIECES)
JOBS = [(0, 0)] + [job for f in range(1, FT) for job in ((f, 0), (f - 1, 1))] + [(FT - 1, 1)]
NJ = len(JOBS)
JOB_AT = {job: n for n, job in enumerate(JOBS)}
NG1 = B * GB


def ffn_and_projections(nc, x, wq, wk, wv, bo, x_cols, wg, wu, b1, b3, wd, a2, b2, q_parts, k_parts, v_dram, y_dram, ident):
    ctx = ExitStack()
    with ctx:
        def sb(name, shape, dt=F32):
            return ctx.enter_context(nc.sbuf_tensor(name, shape, dt))

        def sem(name):
            return ctx.enter_context(nc.semaphore(name))

        wq_sb, wk_sb, wv_sb = (sb(n, [P, DT, D]) for n in ("wq_sb", "wk_sb", "wv_sb"))
        cols_sb = sb("cols_sb", [P, DT, UW])
        wg_sb, wu_sb = sb("wg_sb", [P, DT, F]), sb("wu_sb", [P, DT, F])
        b1_sb, b3_sb = sb("b1_sb", [P, F]), sb("b3_sb", [P, F])
        wd_sb, a2_sb = sb("wd_sb", [P, FT, D]), sb("a2_sb", [P, FT, ER])
        b2_sb = sb("b2_sb", [P, D])
        bo_sb = sb("bo_sb", [P, D])
        expert_of = sb("expert_of", [P, ER])
        eps_col = sb("eps_col", [P, 1])

        x_sb = sb("x_sb", [P, GT, D])
        bn = sb("bn", [P, GT, 6])
        mean_var = sb("mean_var", [P, GT, 2])
        std, rstd = sb("std", [P, GT]), sb("rstd", [P, GT])
        xn = sb("xn", [P, GT, D])
        qk_f = sb("qk_f", [P, 2, G])
        rest = sb("rest", [P, 2, G])
        parts = sb("parts", [P, 2 * DT, NP, G], BF16)
        v_sb = sb("v_sb", [P, GT, D])
        logits = sb("logits", [P, GT, E])
        top = sb("top", [P, GT, 8])
        top_at = sb("top_at", [P, GT, 8], U32)
        chosen = sb("chosen", [P, GT, 2])
        dlogit, edl, den = sb("dlogit", [P, GT]), sb("edl", [P, GT]), sb("den", [P, GT])
        rw = sb("rw", [P, 2, GT])
        mask = sb("mask", [P, 2, GT, ER])
        weight = sb("weight", [P, 2, GT, P])
        uT = sb("uT", [P, 2, G])
        dmask = sb("dmask", [P, G])
        xnT = [sb(f"xnT{i}", [P, DT, G]) for i in range(2)]
        maskT = [sb(f"maskT{i}", [P, 2, G]) for i in range(2)]
        weightT = [sb(f"weightT{i}", [P, 2, G]) for i in range(2)]
        loraT = [sb(f"loraT{i}", [P, 2, 2, G]) for i in range(2)]
        y_sb = [sb(f"y_sb{i}", [P, GT, D]) for i in range(2)]
        silu, silu_w = sb("silu", [P, 3, G]), sb("silu_w", [P, 3, G])
        act = sb("act", [P, 2, FT, G])
        both = sb("both", [P, FT, G])
        z_a, z_b, zT = sb("z_a", [P, G]), sb("z_b", [P, G]), sb("zT", [P, G])
        ps = ctx.enter_context(nc.psum_tensor("ps", [P, 8, G], F32))

        weights_in, bo_in, consts, ident_step, scaled = (sem(n) for n in ("weights_in", "bo_in", "consts", "ident_step", "scaled"))
        x_in, x_used = sem("x_in"), sem("x_used")
        bn_done, stats_done, std_done, rstd_done, xn_done = (sem(n) for n in ("bn_done", "stats_done", "std_done", "rstd_done", "xn_done"))
        piece_psum, piece_out = sem("piece_psum"), sem("piece_out")
        part1_done, rest_done, part2_done, parts_done, qk_stored = (sem(n) for n in ("part1_done", "rest_done", "part2_done", "parts_done", "qk_stored"))
        v_stored = sem("v_stored")
        top_done, at_done, chosen_done, dl_done, edl_done, den_done, rw0_done, rw_done = (
            sem(n) for n in ("top_done", "at_done", "chosen_done", "dl_done", "edl_done", "den_done", "rw0_done", "rw_done"))
        mask_done, weight_done, dmask_done, lora_done = (sem(n) for n in ("mask_done", "weight_done", "dmask_done", "lora_done"))
        h_psum, silu_done, silu_w_done, act_done, both_done = (sem(n) for n in ("h_psum", "silu_done", "silu_w_done", "act_done", "both_done"))
        z_psum, zm_done, z_done = sem("z_psum"), sem("zm_done"), sem("z_done")
        y_psum, y_done, y_stored = sem("y_psum"), sem("y_done"), sem("y_stored")

        weight_loads = [(dst[:], src.rearrange("(t p) c -> p t c", p=P)) for dst, src in
                        ((wq_sb, wq), (wk_sb, wk), (wv_sb, wv), (cols_sb, x_cols), (wg_sb, wg), (wu_sb, wu), (wd_sb, wd), (a2_sb, a2))]
        weight_loads += [(b1_sb[:], b1), (b3_sb[:], b3), (b2_sb[:], b2)]
        rows_of = [m.rearrange("b (g t p) d -> (b g) p t d", p=P, t=GT) for m in (x, y_dram, v_dram)]
        x_rows, y_rows, v_rows = rows_of
        block = ctx.enter_context(nc.Block())

        def all_groups(engine, prepare, work):
            prepare(0, 0)
            with engine.Fori(0, NG1 // 2 - 1) as pair:
                for i in range(2):
                    work(2 * pair + i, i, True, True)
            work(NG1 - 2, 0, True, False)
            work(NG1 - 1, 1, False, False)

        @block.sync
        def _(sp):
            def load_x(g):
                sp.dma_start(x_sb[:], x_rows[bass.ds(g, 1)].rearrange("a p t d -> (a p) t d")).then_inc(x_in, 16)

            def store_prepared(g, i):
                for m in range(2 * DT):
                    sp.wait_ge(parts_done, g * (2 * DT) + m + 1)
                    dst = q_parts if m < DT else k_parts
                    heads = slice((m % DT) * H // DT, (m % DT + 1) * H // DT)
                    for a in range(NP):
                        sp.dma_start(dst[heads, a, :, bass.ds(g * G, G)], parts[:, m, a, :]).then_inc(qk_stored, 16)
                sp.wait_ge(piece_out, g * NPC + NPC)
                sp.dma_start(v_rows[bass.ds(g, 1)].rearrange("a p t d -> (a p) t d"), v_sb[:]).then_inc(v_stored, 16)

            def prepare(g, i):
                load_x(0)
                sp.wait_ge(x_used, 1)
                load_x(1)
                store_prepared(g, i)

            def work(g, i, prepares, loads):
                if loads:
                    sp.wait_ge(x_used, g + 2)
                    load_x(g + 2)
                if prepares:
                    store_prepared(g + 1, 1 - i)
                sp.wait_ge(y_done, g * 2 + 4)
                sp.dma_start(y_rows[bass.ds(g, 1)].rearrange("a p t d -> (a p) t d"), y_sb[i][:]).then_inc(y_stored, 16)

            sp.dma_start(bo_sb[:], bo.rearrange("(a n) -> a n", a=1).to_broadcast([P, D])).then_inc(bo_in, 16)
            all_groups(sp, prepare, work)
            sp.wait_ge(qk_stored, 16 * QK_STORES * NG1 + 16)
            sp.wait_ge(v_stored, 16 * NG1 + 16)
            sp.wait_ge(y_stored, 16 * NG1 + 32)

        @block.gpsimd
        def _(pool):
            nc.gpsimd.memset(ident[:], 0.0).then_inc(ident_step, 1)
            pool.wait_ge(ident_step, 1)
            nc.gpsimd.affine_select(out=ident[:], in_=ident[:], compare_op=ALU.not_equal, fill=1.0, base=0,
                                    pattern=[[-1, P]], channel_multiplier=1).then_inc(consts, 1)
            nc.gpsimd.iota(expert_of[:], pattern=[[1, E], [0, R]], base=0, channel_multiplier=0,
                           allow_small_or_imprecise_dtypes=True).then_inc(consts, 1)
            nc.gpsimd.memset(eps_col[:], EPS).then_inc(consts, 1)
            for free, n in ((y_stored, 32), (qk_stored, 16), (v_stored, 16), (y_done, 2), (act_done, NJ), (silu_w_done, NJ), (lora_done, 1), (zm_done, 2)):
                pool.sem_inc(free, n)

            def work(g, i, prepares, loads):
                for n, (f, s) in enumerate(JOBS):
                    pool.wait_ge(act_done, g * NJ + NJ + n - 2)
                    pool.wait_ge(silu_done, g * NJ + n + 1)
                    nc.gpsimd.tensor_tensor(silu_w[:, n % 3, :], silu[:, n % 3, :], weightT[i][:, s, :], ALU.mult).then_inc(silu_w_done, 1)
                    if s == 1 and f >= 1:
                        sum_slots(g, f - 1)
                sum_slots(g, FT - 1)

            def sum_slots(g, f):
                pool.wait_ge(act_done, g * NJ + NJ + JOB_AT[f, 1] + 1)
                pool.wait_ge(y_done, g * 2 + 2)
                nc.gpsimd.tensor_tensor(both[:, f, :], act[:, 0, f, :], act[:, 1, f, :], ALU.add).then_inc(both_done, 1)

            all_groups(pool, lambda g, i: None, work)

        @block.scalar
        def _(act_e):
            for dst, src in weight_loads:
                act_e.dma_start(dst, src).then_inc(weights_in, 16)
            act_e.wait_ge(consts, 3)
            copy = lambda dst, src: nc.scalar.activation(dst, src, ACT.Copy)

            def std_dev(g):
                act_e.wait_ge(stats_done, g + 1)
                nc.scalar.activation(std[:], mean_var[:, :, 1], ACT.Sqrt, bias=eps_col[:]).then_inc(std_done, 1)

            def piece(g, i, k):
                name = PIECES[k]
                what, t = name[:-1], int(name[-1]) if name[-1].isdigit() else 0
                bank = ps[:, 6 + k % 2, :]
                if name == "q0":
                    act_e.wait_ge(dl_done, g + 1)
                    nc.scalar.activation(edl[:], dlogit[:], ACT.Exp).then_inc(edl_done, 1)
                if name == "v0":
                    act_e.wait_ge(v_stored, g * 16 + 16)
                if what in ("q", "k"):
                    m = t + (DT if what == "k" else 0)
                    if m >= 2:
                        act_e.wait_ge(rest_done, g * (2 * DT) + m - 1)
                if name == "u0":
                    act_e.wait_ge(lora_done, g + 1)
                act_e.wait_ge(piece_psum, g * NPC + k + 1)
                if what == "xT":
                    last = copy(xnT[i][:, t, :], bank)
                elif name == "logits":
                    last = copy(logits[:].rearrange("p t e -> p (t e)"), bank[:, 0:GT * E])
                elif what == "u":
                    last = copy(uT[:, t, :], bank)
                elif what in ("q", "k"):
                    last = copy(qk_f[:, m % 2, :], bank)
                elif what == "mask":
                    last = copy(maskT[i][:, t, :], bank)
                elif what == "weight":
                    last = copy(weightT[i][:, t, :], bank)
                else:
                    last = copy(v_sb[:, 2 * t:2 * t + 2, :].rearrange("p t d -> p (t d)"), bank)
                last.then_inc(piece_out, 1)

            def prepare(g, i):
                std_dev(g)
                for k in range(NPC):
                    piece(g, i, k)

            def work(g, i, prepares, loads):
                if prepares:
                    std_dev(g + 1)
                for n, (f, s) in enumerate(JOBS):
                    act_e.wait_ge(silu_w_done, g * NJ + NJ + n - 2)
                    act_e.wait_ge(h_psum, g * NJ + n + 1)
                    nc.scalar.activation(silu[:, n % 3, :], ps[:, 2 * (f % 3), :], ACT.Silu).then_inc(silu_done, 1)
                    if prepares and n >= 1:
                        piece(g + 1, 1 - i, n - 1)

            all_groups(act_e, prepare, work)

        @block.vector
        def _(dve):
            dve.wait_ge(weights_in, 16 * len(weight_loads))
            for w in (b1_sb, b3_sb, b2_sb):
                nc.vector.tensor_scalar(w[:], w[:], LORA_SCALE, None, ALU.mult).then_inc(scaled, 1)
            dve.wait_ge(bo_in, 16)
            dve.wait_ge(consts, 3)

            def layer_norm(g, i):
                dve.wait_ge(x_in, g * 16 + 16)
                for t in range(GT):
                    nc.vector.bn_stats(bn[:, t, :], x_sb[:, t, :]).then_inc(bn_done, 1)
                dve.wait_ge(bn_done, g * GT + GT)
                nc.vector.memset(rstd[:], 0.0)
                for t in range(GT):
                    last = nc.vector.bn_aggr(mean_var[:, t, :], bn[:, t, :])
                last.then_inc(stats_done, 1)
                dve.wait_ge(std_done, g + 1)
                nc.vector.reciprocal(rstd[:], std[:]).then_inc(rstd_done, 1)
                dve.wait_ge(rstd_done, g + 1)
                for t in range(GT):
                    last = nc.vector.tensor_scalar(xn[:, t, :], x_sb[:, t, :], mean_var[:, t, 0:1], rstd[:, t:t + 1], ALU.subtract, ALU.mult)
                last.then_inc(xn_done, 1)

            def start_y(g, i):
                dve.wait_ge(y_stored, g * 16 + 16)
                nc.vector.tensor_tensor(y_sb[i][:], x_sb[:], bo_sb[:].unsqueeze(1).to_broadcast([P, GT, D]), ALU.add).then_inc(x_used, 1)

            def split(g, m, out):
                if m == 0:
                    dve.wait_ge(qk_stored, g * (16 * QK_STORES) + 16)
                dve.wait_ge(piece_out, g * NPC + out + 1)
                nc.vector.tensor_copy(parts[:, m, 0, :], qk_f[:, m % 2, :]).then_inc(part1_done, 1)
                dve.wait_ge(part1_done, g * (2 * DT) + m + 1)
                nc.vector.tensor_tensor(rest[:, m % 2, :], qk_f[:, m % 2, :], parts[:, m, 0, :], ALU.subtract).then_inc(rest_done, 1)
                dve.wait_ge(rest_done, g * (2 * DT) + m + 1)
                nc.vector.tensor_copy(parts[:, m, 1, :], rest[:, m % 2, :]).then_inc(part2_done, 1)
                dve.wait_ge(part2_done, g * (2 * DT) + m + 1)
                nc.vector.tensor_tensor(parts[:, m, 2, :], rest[:, m % 2, :], parts[:, m, 1, :], ALU.subtract).then_inc(parts_done, 1)

            def experts(g):
                for t in range(GT):
                    nc.vector.max(top[:, t, :], logits[:, t, :]).then_inc(top_done, 1)
                dve.wait_ge(top_done, g * GT + GT)
                nc.vector.tensor_tensor(dlogit[:], top[:, :, 1], top[:, :, 0], ALU.subtract).then_inc(dl_done, 1)
                for t in range(GT):
                    last = nc.vector.max_index(top_at[:, t, :], top[:, t, :], logits[:, t, :])
                last.then_inc(at_done, 1)
                dve.wait_ge(at_done, g + 1)
                nc.vector.tensor_copy(chosen[:], top_at[:, :, 0:2]).then_inc(chosen_done, 1)

            def masks(g):
                dve.wait_ge(chosen_done, g + 1)
                for s in range(2):
                    for t in range(GT):
                        last = nc.vector.tensor_scalar(mask[:, s, t, :], expert_of[:], chosen[:, t, s:s + 1], None, ALU.is_equal)
                last.then_inc(mask_done, 1)

            def weights(g):
                dve.wait_ge(edl_done, g + 1)
                nc.vector.tensor_scalar(den[:], edl[:], 1.0, None, ALU.add).then_inc(den_done, 1)
                dve.wait_ge(den_done, g + 1)
                nc.vector.reciprocal(rw[:, 0, :], den[:]).then_inc(rw0_done, 1)
                dve.wait_ge(rw0_done, g + 1)
                nc.vector.tensor_tensor(rw[:, 1, :], edl[:], rw[:, 0, :], ALU.mult).then_inc(rw_done, 1)
                dve.wait_ge(rw_done, g + 1)
                nc.vector.tensor_copy(weight[:].rearrange("p s t c -> p (s t) c"),
                                      rw[:].rearrange("p s t -> p (s t)").unsqueeze(2).to_broadcast([P, 2 * GT, P])).then_inc(weight_done, 1)

            def masked(g, i):
                dve.wait_ge(piece_out, g * NPC + PIECES.index("mask1") + 1)
                nc.vector.tensor_tensor(dmask[:], maskT[i][:, 1, :], maskT[i][:, 0, :], ALU.subtract).then_inc(dmask_done, 1)
                for a in range(2):
                    nc.vector.tensor_tensor(loraT[i][:, 0, a, :], uT[:, a, :], maskT[i][:, 0, :], ALU.mult)
                dve.wait_ge(dmask_done, g + 1)
                for a in range(2):
                    last = nc.vector.tensor_tensor(loraT[i][:, 1, a, :], uT[:, a, :], dmask[:], ALU.mult)
                last.then_inc(lora_done, 1)

            steps = {3: start_y, 5: lambda g, i: experts(g), 6: lambda g, i: masks(g), 7: lambda g, i: split(g, 0, PIECES.index("q0")),
                     8: lambda g, i: weights(g), 9: lambda g, i: split(g, 1, PIECES.index("q1")), 11: masked,
                     14: lambda g, i: split(g, 2, PIECES.index("k0")), 15: lambda g, i: split(g, 3, PIECES.index("k1"))}

            def prepare(g, i):
                layer_norm(g, i)
                for n in sorted(steps):
                    if n == 5:
                        dve.wait_ge(piece_out, g * NPC + PIECES.index("logits") + 1)
                        nc.vector.memset(den[:], 0.0)
                    steps[n](g, i)

            def work(g, i, prepares, loads):
                if prepares:
                    layer_norm(g + 1, 1 - i)
                for n, (f, s) in enumerate(JOBS):
                    if prepares and n == 5:
                        dve.wait_ge(piece_out, (g + 1) * NPC + PIECES.index("logits") + 1)
                    dve.wait_ge(silu_w_done, g * NJ + NJ + n + 1)
                    nc.vector.tensor_tensor(act[:, s, f, :], ps[:, 2 * (f % 3) + 1, :], silu_w[:, n % 3, :], ALU.mult).then_inc(act_done, 1)
                    if prepares and n in steps:
                        steps[n](g + 1, 1 - i)
                for s, z in enumerate((z_a, z_b)):
                    dve.wait_ge(z_psum, g * 2 + s + 1)
                    nc.vector.tensor_tensor(z[:], ps[:, 4 + s, :], maskT[i][:, s, :], ALU.mult).then_inc(zm_done, 1)
                dve.wait_ge(zm_done, g * 2 + 4)
                nc.vector.tensor_tensor(zT[:], z_a[:], z_b[:], ALU.add).then_inc(z_done, 1)
                for k in range(2):
                    dve.wait_ge(y_psum, g * 2 + k + 1)
                    y = y_sb[i][:, 2 * k:2 * k + 2, :].rearrange("p t d -> p (t d)")
                    nc.vector.tensor_tensor(y, ps[:, 6 + k, :], y, ALU.add).then_inc(y_done, 1)

            all_groups(dve, prepare, work)

        @block.tensor
        def _(pe):
            mm = nc.tensor.matmul
            pe.wait_ge(weights_in, 16 * len(weight_loads))
            pe.wait_ge(scaled, 3)
            pe.wait_ge(consts, 3)

            def piece(g, i, k, first=False):
                name = PIECES[k]
                what, t = name[:-1], int(name[-1]) if name[-1].isdigit() else 0
                bank = ps[:, 6 + k % 2, :]
                if k < 2 and not first:
                    pe.wait_ge(y_done, g * 2 + k - 1)
                elif k >= 2:
                    pe.wait_ge(piece_out, g * NPC + k - 1)
                if what == "xT":
                    pe.wait_ge(xn_done, g + 1)
                    for n in range(GT):
                        last = nc.tensor.transpose(bank[:, n * P:(n + 1) * P], xn[:, n, t * P:(t + 1) * P], ident[:])
                elif name == "logits":
                    pe.wait_ge(piece_out, g * NPC + PIECES.index("xT1") + 1)
                    for n in range(GT):
                        for d in range(DT):
                            last = mm(bank[:, n * E:(n + 1) * E], xnT[i][:, d, n * P:(n + 1) * P], cols_sb[:, d, 2 * ER:UW], start=(d == 0), stop=(d == DT - 1))
                elif what in ("u", "q", "k"):
                    w = {"u": cols_sb, "q": wq_sb, "k": wk_sb}[what]
                    for d in range(DT):
                        last = mm(bank, w[:, d, t * P:(t + 1) * P], xnT[i][:, d, :], start=(d == 0), stop=(d == DT - 1))
                elif what in ("mask", "weight"):
                    pe.wait_ge(mask_done if what == "mask" else weight_done, g + 1)
                    src = mask if what == "mask" else weight
                    for n in range(GT):
                        last = nc.tensor.transpose(bank[:, n * P:(n + 1) * P], src[:, t, n, :], ident[:])
                else:
                    for n in range(2):
                        for d in range(DT):
                            tile = 2 * t + n
                            last = mm(bank[:, n * D:(n + 1) * D], xnT[i][:, d, tile * P:(tile + 1) * P], wv_sb[:, d, :], start=(d == 0), stop=(d == DT - 1))
                last.then_inc(piece_psum, 1)

            def prepare(g, i):
                for k in range(NPC):
                    piece(g, i, k, first=True)

            def work(g, i, prepares, loads):
                pe.wait_ge(lora_done, g + 2)
                for n, (f, s) in enumerate(JOBS):
                    gate, up = ps[:, 2 * (f % 3), :], ps[:, 2 * (f % 3) + 1, :]
                    cols = slice(f * P, (f + 1) * P)
                    if s == 0:
                        if f >= 3:
                            pe.wait_ge(act_done, g * NJ + NJ + JOB_AT[f - 3, 1] + 1)
                        else:
                            pe.wait_ge(act_done, g * NJ + NJ)
                            if f == 2:
                                pe.wait_ge(zm_done, g * 2 + 2)
                        for w, b, out, a in ((wg_sb, b1_sb, gate, 0), (wu_sb, b3_sb, up, 1)):
                            for d in range(DT):
                                mm(out, w[:, d, cols], xnT[i][:, d, :], start=(d == 0), stop=False)
                            last = mm(out, b[:, cols], loraT[i][:, 0, a, :], start=False, stop=True)
                    else:
                        pe.wait_ge(act_done, g * NJ + NJ + JOB_AT[f, 0] + 1)
                        for b, out, a in ((b1_sb, gate, 0), (b3_sb, up, 1)):
                            last = mm(out, b[:, cols], loraT[i][:, 1, a, :], start=False, stop=True, skip_group_check=True)
                    last.then_inc(h_psum, 1)
                    if prepares and n >= 1:
                        piece(g + 1, 1 - i, n - 1)
                pe.wait_ge(act_done, g * NJ + NJ + JOB_AT[FT - 3, 1] + 1)
                for s in range(2):
                    for f in range(FT):
                        if f >= FT - 2:
                            pe.wait_ge(act_done, g * NJ + NJ + JOB_AT[f, s] + 1)
                        last = mm(ps[:, 4 + s, :], a2_sb[:, f, :], act[:, s, f, :], start=(f == 0), stop=(f == FT - 1))
                    last.then_inc(z_psum, 1)
                if prepares:
                    pe.wait_ge(piece_out, (g + 1) * NPC + NPC)
                pe.wait_ge(both_done, g * FT + FT)
                for n in range(GT):
                    out, tile = ps[:, 6 + n // 2, (n % 2) * D:(n % 2 + 1) * D], slice(n * P, (n + 1) * P)
                    for f in range(FT):
                        mm(out, both[:, f, tile], wd_sb[:, f, :], start=(f == 0), stop=False)
                    if n == 0:
                        pe.wait_ge(z_done, g + 1)
                    last = mm(out, zT[:, tile], b2_sb[:], start=False, stop=True)
                    if n % 2:
                        last.then_inc(y_psum, 1)

            all_groups(pe, prepare, work)


QT = N // P
SLOT = 1024
CHUNK = 512
CB = CHUNK // P
QW = 32
ROWS = 8 * HD
MASKED = -1e30
SM_SCALE = 1.0 / HD ** 0.5
TABLE = P - 1 + N
OG = G // P


def attention(nc, q_parts, k_parts, v_dram, table, w, v, v_all, ident):
    ctx = ExitStack()
    with ctx:
        def sb(name, shape, dt=F32):
            return ctx.enter_context(nc.sbuf_tensor(name, shape, dt))

        def sem(name):
            return ctx.enter_context(nc.semaphore(name))

        DC = N // P
        zero = sb("zero", [P, P])
        factor = sb("factor", [P, N])
        factor_next = sb("factor_next", [P, N])
        NROW = 8
        hide = sb("hide", [P, P])
        w_neg, v_bc, ev1 = sb("w_neg", [P, H]), sb("v_bc", [P, H]), sb("ev1", [P, H])
        qx = [sb(f"qx{j}", [P, N], BF16) for j in range(B)]
        kx = [sb(f"kx{j}", [P, N], BF16) for j in range(B)]
        vx = [sb(f"vx{j}", [P, QT, QW]) for j in range(B)]
        none = sb("none", [P, P], BF16)
        rows = [sb(f"rows{i}", [P, N]) for i in range(NROW)]
        factors = rows[0][:, 0:H * DC].rearrange("p (h c) -> p h c", h=H)
        dist = rows[1][:, 0:DC]
        top = sb("row_max", [P, 8])
        unused = sb("unused", [P, 8])
        probs = [sb(f"probs{i}", [P, CHUNK]) for i in range(4)]
        o_parts = [sb(f"o_parts{i}", [P, G]) for i in range(2)]
        fold = sb("fold", [P, QW])
        inv = sb("inv", [P, 2, OG])
        ps = ctx.enter_context(nc.psum_tensor("ps_attn", [P, 8, G], F32))

        const_step, consts, wv_in, wv_done, ev_done = (sem(n) for n in ("const_step", "a_consts", "wv_in", "wv_done", "ev_done"))
        decay_done, factor_step, table_stored = sem("decay_done"), sem("factor_step"), sem("table_stored")
        factor_in, factor_taken, spare_stored = sem("factor_in"), sem("factor_taken"), sem("spare_stored")
        qk_in = [sem(f"qk_in{j}") for j in range(B)]
        v_in, vx_done = sem("v_in"), sem("vx_done")
        s_psum, scaled = sem("s_psum"), sem("s_scaled")
        row_done, diag_done = sem("row_done"), sem("diag_done")
        t_psum, probs_done = sem("t_psum"), sem("probs_done")
        pv_done = sem("pv_done")
        o_done, f_psum = sem("o_done"), sem("f_psum")
        inv_done, normed = sem("inv_done"), sem("normed")

        tiles = [jt for b in range(0, B, 2) for i in range(QT) for jt in ((b, QT - 1 - i), (b + 1, i))]
        slots, chunks = [], []
        for n, (j, t) in enumerate(tiles):
            keys = (t + 1) * P
            slots += [(n, k, min(SLOT, keys - k)) for k in range(0, keys, SLOT)]
            chunks += [(n, kb, min(CB, t + 1 - kb)) for kb in range(0, t + 1, CB)]
        NT, NS, NC, NG = len(tiles), len(slots), len(chunks), len(tiles) // OG
        assert NS % 2 == 0 and NC % 4 == 0 and NT % 2 == 0 and NG % 2 == 0
        slots_of = [[c for c, s in enumerate(slots) if s[0] == n] for n in range(NT)]
        chunks_of = [[c for c, s in enumerate(chunks) if s[0] == n] for n in range(NT)]
        last_chunk = [chunks_of[n][-1] for n in range(NT)]
        last_of = [max(n for n in range(NT) if tiles[n][0] == j) for j in range(B)]
        first_of = [min(n for n in range(NT) if tiles[n][0] == j) for j in range(B)]
        tile_of = lambda c: c // NS * NT + slots[c % NS][0]
        ends_tile = lambda c: tile_of(c + 1) != tile_of(c)
        end_slot = lambda n: n // NT * NS + slots_of[n % NT][-1]
        first_key_block = lambda c: c // NS * sum(kn for _, _, kn in slots) // P + sum(kn for _, _, kn in slots[:c % NS]) // P
        LAG_O, LAG_F = 3, 4
        LAG_P = 2
        evac_after = {min(last_chunk[OG * g + OG - 1] + LAG_O, NC - 1): g for g in range(NG)}
        fold_after = {min(last_chunk[OG * g + OG - 1] + LAG_F, NC - 1): g for g in range(NG)}
        LEAD = 18
        AHEAD = next(c for c in range(NS) if first_key_block(c) > LEAD)
        slots_after, made, t_blocks = [[] for _ in range(NC + 1)], AHEAD, 0
        norm_before = {}
        for k in range(NC + 1):
            tile = chunks[k][0] if k < NC else NT
            while made < NS + AHEAD and (made <= end_slot(tile) + 1 or k == NC
                                         or first_key_block(made) <= t_blocks + LEAD and tile_of(made - 2) - NROW < tile):
                slots_after[k].append(made)
                made += 1
            t_blocks += chunks[k][2] if k < NC else 0
            g = fold_after.get(k - 1 - LAG_P)
            if g is not None and g < NG - 1:
                norm_before.setdefault(min(max(made, end_slot(chunks[k - 1][0]) + 2), NS + AHEAD), []).append(g)
        norm_before.setdefault(NS + AHEAD, []).append(NG - 1)
        LOADS = 5
        credits = [(s_psum, NS), (scaled, 2), (t_psum, NC), (probs_done, 2), (pv_done, NC), (f_psum, 2), (normed, 2)]
        assert len(probs) == 4

        block = ctx.enter_context(nc.Block())

        @block.sync
        def _(sp):
            sp.dma_start(w_neg[:], w.rearrange("(a n) -> a n", a=1).to_broadcast([P, H])).then_inc(wv_in, 16)
            sp.dma_start(v_bc[:], v.rearrange("(a n) -> a n", a=1).to_broadcast([P, H])).then_inc(wv_in, 16)
            for b in range(B):
                sp.dma_start(v_all[:, b * QT:(b + 1) * QT, :], v_dram[b].rearrange("(t p) d -> p t d", p=P)).then_inc(v_in, 16)
            for m in (q_parts, k_parts):
                sp.dma_start(m[H].rearrange("a d t -> (a d) t"), m[0].rearrange("a d t -> (a d) t")).then_inc(spare_stored, 16)
            sp.wait_ge(factor_step, 3)
            for dst, src in [(table[0:H, P - 1:TABLE], factors), (table[H:H + 1, P - 1:TABLE], factors[:, 0:1, :])]:
                sp.dma_start(dst.rearrange("h (p c) -> p h c", p=P), src).then_inc(table_stored, 16)
            sp.dma_start(table[:, 0:P - 1], zero[0:H + 1, 0:P - 1]).then_inc(table_stored, 16)

            def load_factor(h):
                sp.dma_start(factor_next[:], bass.AP(tensor=table.tensor, offset=h * TABLE, ap=[[1, P], [1, N]])).then_inc(factor_in, 16)

            def load_qk(h, j):
                q = q_parts[bass.ds(h, 1), :, :, j * N:(j + 1) * N].rearrange("h a d t -> (h a d) t")
                k = k_parts[bass.ds(h, 1), :, :, j * N:(j + 1) * N].rearrange("h a d t -> (h a) d t")
                sp.dma_start(qx[j][0:2 * NP * HD, :], q.unsqueeze(0).to_broadcast([2, NP * HD, N])).then_inc(qk_in[j], 16)
                sp.dma_start(qx[j][2 * NP * HD:ROWS, :], q[0:2 * HD, :]).then_inc(qk_in[j], 16)
                for a, (r0, r1) in enumerate(((0, 3), (3, 6), (6, 8))):
                    sp.dma_start(kx[j][r0 * HD:r1 * HD, :], k[a:a + 1].to_broadcast([r1 - r0, HD, N])).then_inc(qk_in[j], 16)

            for j in range(B):
                load_qk(0, j)
            sp.wait_ge(table_stored, 48)
            load_factor(0)
            sp.wait_ge(spare_stored, 32)
            with sp.Fori(0, H) as h:
                sp.wait_ge(factor_taken, h + 1)
                load_factor(h + 1)
                for j in range(B):
                    sp.wait_ge(s_psum, h * NS + NS + slots_of[last_of[j]][-1] + 1)
                    load_qk(h + 1, j)
            for j in range(B):
                sp.wait_ge(qk_in[j], 16 * LOADS * (H + 1))
            sp.wait_ge(factor_in, 16 * (H + 1))

        @block.gpsimd
        def _(pool):
            nc.gpsimd.iota(dist, pattern=[[1, DC]], base=0, channel_multiplier=DC, allow_small_or_imprecise_dtypes=True).then_inc(consts, 1)
            nc.gpsimd.memset(zero[:], 0.0).then_inc(const_step, 1)
            nc.gpsimd.memset(hide[:], 0.0).then_inc(const_step, 1)
            nc.gpsimd.memset(fold[:], 0.0).then_inc(const_step, 1)
            nc.gpsimd.memset(none[:], 0.0).then_inc(consts, 1)
            for j in range(B):
                nc.gpsimd.memset(vx[j][:], 0.0).then_inc(const_step, 1)
            pool.wait_ge(const_step, 3 + B)
            for j in range(B):
                nc.gpsimd.memset(vx[j][:, :, HD:HD + 1], 1.0).then_inc(consts, 1)
            nc.gpsimd.affine_select(out=hide[:], in_=hide[:], compare_op=ALU.is_ge, fill=MASKED, base=0,
                                    pattern=[[-1, P]], channel_multiplier=1).then_inc(consts, 1)
            for i in range(CB):
                nc.gpsimd.affine_select(out=fold[:], in_=fold[:], compare_op=ALU.not_equal, fill=1.0, base=-QW * i,
                                        pattern=[[-1, QW]], channel_multiplier=1).then_inc(const_step, 1)
                pool.wait_ge(const_step, 4 + B + i)
            for free, n in credits:
                pool.sem_inc(free, n)
            pool.wait_ge(consts, 3 + B)
            pool.sem_inc(consts, 1)
            with pool.Fori(0, H) as h:
                for n, (j, t) in enumerate(tiles):
                    if n == first_of[j]:
                        pool.wait_ge(v_in, 16 * B)
                        pool.wait_ge(pv_done, h * NC + last_chunk[last_of[j]] + 1)
                    pool.wait_ge(row_done, h * NT + n + 1)
                    diag = rows[n % NROW][:, t * P:(t + 1) * P]
                    nc.gpsimd.tensor_tensor(diag, diag, hide[:], ALU.add).then_inc(diag_done, 1)
                    if n == first_of[j]:
                        nc.gpsimd.tensor_copy(vx[j][:, :, 0:HD], v_all[:, bass.ds(j * QT, QT), bass.ds(h * HD, HD)]).then_inc(vx_done, 1)

        @block.scalar
        def _(act_e):
            act_e.wait_ge(wv_in, 32)
            nc.scalar.activation(ev1[:], v_bc[:], ACT.Exp).then_inc(ev_done, 1)
            act_e.wait_ge(wv_done, 2)
            act_e.wait_ge(consts, 4 + B)
            for h in range(H):
                nc.scalar.activation(factors[:, h, :], dist, ACT.Exp, scale=w_neg[:, h:h + 1], bias=v_bc[:, h:h + 1]).then_inc(decay_done, 1)
            with act_e.Fori(0, H) as h:
                for c, (n, kb, m) in enumerate(chunks):
                    act_e.wait_ge(pv_done, h * NC + NC + c - 3)
                    act_e.wait_ge(t_psum, h * NC + NC + c + 1)
                    nc.scalar.activation(probs[c % 4][:, 0:m * P], ps[:, 4 + c % 2, 0:m * P], ACT.Exp, scale=SM_SCALE).then_inc(probs_done, 1)
                    if c in evac_after:
                        g = evac_after[c]
                        act_e.wait_ge(f_psum, h * NG + g + 1)
                        act_e.wait_ge(pv_done, h * NC + NC + last_chunk[OG * g + OG - 1] + 1)
                        nc.scalar.activation(o_parts[g % 2][:], ps[:, 6 + g % 2, :], ACT.Copy).then_inc(o_done, 1)

        @block.vector
        def _(dve):
            dve.wait_ge(wv_in, 32)
            nc.vector.tensor_scalar(w_neg[:], w_neg[:], -1.0, None, ALU.mult).then_inc(wv_done, 1)
            dve.wait_ge(ev_done, 1)
            nc.vector.tensor_scalar(ev1[:], ev1[:], 1.0, None, ALU.add).then_inc(wv_done, 1)
            dve.wait_ge(consts, 4 + B)
            dve.wait_ge(wv_done, 2)
            dve.wait_ge(decay_done, H)
            nc.vector.tensor_scalar(factors, factors, 1.0, None, ALU.add).then_inc(factor_step, 1)
            dve.wait_ge(factor_step, 1)
            nc.vector.reciprocal(factors, factors).then_inc(factor_step, 1)
            dve.wait_ge(factor_step, 2)
            nc.vector.tensor_tensor(factors, factors, ev1[:].unsqueeze(2).to_broadcast([P, H, DC]), ALU.mult).then_inc(factor_step, 1)

            def take_factor(h):
                dve.wait_ge(factor_in, h * 16 + 16)
                dve.wait_ge(scaled, h * NS + 2)
                nc.vector.tensor_copy(factor[:], factor_next[:]).then_inc(factor_taken, 1)

            def invert(h, g):
                dve.wait_ge(f_psum, h * NG + g + 3)
                nc.vector.reciprocal(inv[:, g % 2, :], ps[:, 6 + g % 2, 0:OG * QW].rearrange("p (t c) -> p t c", c=QW)[:, :, HD]).then_inc(inv_done, 1)

            def normalise(h, g):
                o = ps[:, 6 + g % 2, 0:OG * QW].rearrange("p (t c) -> p t c", c=QW)
                dve.wait_ge(inv_done, h * NG + g + 1)
                for i in range(2):
                    order = slice(OG - 2, None, -2) if i == 0 else slice(1, None, 2)
                    j = tiles[OG * g + i][0]
                    first = min(t for b, t in tiles[OG * g:OG * g + OG] if b == j)
                    ins = nc.vector.tensor_tensor(v_all[:, bass.ds(j * QT + first, OG // 2), bass.ds(h * HD, HD)], o[:, order, 0:HD],
                                                  inv[:, g % 2, order].unsqueeze(2).to_broadcast([P, OG // 2, HD]), ALU.mult)
                ins.then_inc(normed, 1)

            def less_max(h, n, c):
                t = tiles[n % NT][1]
                row = rows[n % NROW][:, 0:(t + 1) * P]
                dve.wait_ge(scaled, h * NS + c + 3)
                nc.vector.tensor_scalar(row, row, 0.0, top[:, c % 8:c % 8 + 1], ALU.max, ALU.subtract).then_inc(row_done, 1)

            def scale(h, c):
                n, k0, kn = tile_of(c), slots[c % NS][1], slots[c % NS][2]
                if c % NS == 0:
                    take_factor(h + c // NS)
                dve.wait_ge(s_psum, h * NS + NS + c + 1)
                if k0:
                    dve.wait_ge(scaled, h * NS + c + 2)
                else:
                    old = n - NROW + NT
                    dve.wait_ge(t_psum, h * NC + old // NT * NC + last_chunk[old % NT] + 1)
                if c % NS == 0:
                    dve.wait_ge(factor_taken, h + c // NS + 1)
                nc.vector.memset(unused[:, c % 8:c % 8 + 1], 0.0)
                at_k0 = tiles[n % NT][1] * P + P - 1 - k0
                row = factor[:, at_k0::-1] if at_k0 == kn - 1 else factor[:, at_k0:at_k0 - kn:-1]
                so_far = top[:, (c - 1) % 8:(c - 1) % 8 + 1] if k0 else 0.0
                nc.vector.tensor_tensor_reduce(out=rows[n % NROW][:, k0:k0 + kn], in0=ps[:, 2 * (c % 2):2 * (c % 2) + 2, :].rearrange("p a b -> p (a b)")[:, 0:kn],
                                               in1=row, scale=1.0, scalar=so_far,
                                               op0=ALU.mult, op1=ALU.max, accum_out=top[:, c % 8:c % 8 + 1]).then_inc(scaled, 1)

            def tile_behind(h, c):
                if c > 0 and ends_tile(c - 1):
                    less_max(h, tile_of(c - 1), c - 1)

            for c in range(AHEAD):
                scale(0, c)
                tile_behind(0, c)
            with dve.Fori(0, H) as h:
                for c in range(AHEAD, NS + AHEAD):
                    for g in norm_before.get(c, []):
                        invert(h, g)
                    scale(h, c)
                    for g in norm_before.get(c, []):
                        normalise(h, g)
                    tile_behind(h, c)
                for g in norm_before[NS + AHEAD]:
                    invert(h, g)
                    normalise(h, g)

        @block.tensor
        def _(pe):
            mm = nc.tensor.matmul
            pe.wait_ge(consts, 4 + B)

            def scores(h, c):
                h, c = (h + 1, c - NS) if c >= NS else (h, c)
                n, k0, kn = slots[c]
                j, t = tiles[n]
                if n == first_of[j] and k0 == 0:
                    pe.wait_ge(qk_in[j], h * (16 * LOADS) + 16 * LOADS)
                pe.wait_ge(scaled, h * NS + c + 1)
                for i, k in enumerate(range(0, kn, G)):
                    wd = min(G, kn - k)
                    last = mm(ps[:, 2 * (c % 2) + i, 0:wd], qx[j][:, t * P:(t + 1) * P], kx[j][:, k0 + k:k0 + k + wd], start=True, stop=True)
                last.then_inc(s_psum, 1)

            for c in range(AHEAD):
                scores(0, c)
            with pe.Fori(0, H) as h:
                def transposed(c):
                    n, kb, m = chunks[c]
                    pe.wait_ge(row_done, h * NT + n + 1)
                    if c == last_chunk[n]:
                        pe.wait_ge(diag_done, h * NT + n + 1)
                    pe.wait_ge(probs_done, h * NC + c + 1)
                    for i in range(m):
                        last = nc.tensor.transpose(ps[:, 4 + c % 2, i * P:(i + 1) * P], rows[n % NROW][:, (kb + i) * P:(kb + i + 1) * P], ident[:])
                    last.then_inc(t_psum, 1)

                def output(c):
                    n, kb, m = chunks[c]
                    j, t = tiles[n]
                    g = n // OG
                    if kb == 0 and n == first_of[j]:
                        pe.wait_ge(vx_done, h * B + j + 1)
                    if kb == 0 and n % OG == 0:
                        pe.wait_ge(normed, h * NG + g + 1)
                    pe.wait_ge(probs_done, h * NC + c + 3)
                    cols = slice((n % OG) * P, (n % OG + 1) * P)
                    for i in range(CB):
                        o = ps[i * QW:(i + 1) * QW, 6 + g % 2, cols]
                        if i < m:
                            last = mm(o, vx[j][:, kb + i, :], probs[c % 4][:, i * P:(i + 1) * P], start=(kb == 0), stop=(kb + i + CB > t))
                        elif kb == 0:
                            last = mm(o, none[:, 0:QW], none[:], start=True, stop=True)
                    last.then_inc(pv_done, 1)

                def folded(g):
                    pe.wait_ge(o_done, h * NG + g + 1)
                    for i in range(OG):
                        last = mm(ps[:, 6 + g % 2, i * QW:(i + 1) * QW], o_parts[g % 2][:, i * P:(i + 1) * P], fold[:], start=True, stop=True)
                    last.then_inc(f_psum, 1)

                for c in slots_after[0]:
                    scores(h, c)
                for c in range(NC):
                    transposed(c)
                    for s in slots_after[c + 1]:
                        scores(h, s)
                    if c >= LAG_P:
                        output(c - LAG_P)
                        if c - LAG_P in fold_after:
                            folded(fold_after[c - LAG_P])
                for c in range(NC - LAG_P, NC):
                    output(c)
                folded(NG - 1)


def output_projection(nc, wo, y_dram, ctx_all, ident, out):
    ctx = ExitStack()
    with ctx:
        def sb(name, shape, dt=F32):
            return ctx.enter_context(nc.sbuf_tensor(name, shape, dt))

        def sem(name):
            return ctx.enter_context(nc.semaphore(name))

        wo_sb = sb("wo_sb", [P, DT, D])
        y = [sb(f"y{i}", [P, GT, D]) for i in range(2)]
        ctxT = [sb(f"ctxT{i}", [P, DT, G]) for i in range(2)]
        ps = ctx.enter_context(nc.psum_tensor("ps_out", [P, 8, G], F32))
        wo_in, copied = sem("wo_in"), sem("copied")
        y_in = [sem(f"y_in{i}") for i in range(2)]
        stored = [sem(f"stored{i}") for i in range(2)]
        cT_psum, cT_done, a_psum, summed = sem("cT_psum"), sem("cT_done"), sem("a_psum"), sem("summed")
        NGR = B * GB
        y_rows = y_dram.rearrange("b (g t p) d -> (b g) p t d", p=P, t=GT)
        out_rows = out.rearrange("b (g t p) d -> (b g) p t d", p=P, t=GT)
        block = ctx.enter_context(nc.Block())

        @block.sync
        def _(sp):
            sp.dma_start(wo_sb[:], wo.rearrange("(t p) c -> p t c", p=P)).then_inc(wo_in, 16)
            for g in range(2):
                sp.dma_start(y[g][:], y_rows[g]).then_inc(y_in[g], 16)
            for g in range(NGR):
                sp.wait_ge(summed, g + 1)
                sp.dma_start(out_rows[g], y[g % 2][:]).then_inc(stored[g % 2], 16)
                if g + 2 < NGR:
                    sp.wait_ge(stored[g % 2], 16 * (g // 2 + 1))
                    sp.dma_start(y[g % 2][:], y_rows[g + 2]).then_inc(y_in[g % 2], 16)
            for i in range(2):
                sp.wait_ge(stored[i], 16 * (NGR // 2))

        @block.scalar
        def _(act_e):
            for g in range(NGR):
                if g >= 2:
                    act_e.wait_ge(a_psum, g - 1)
                for t in range(DT):
                    act_e.wait_ge(cT_psum, g * DT + t + 1)
                    nc.scalar.activation(ctxT[g % 2][:, t, :], ps[:, 2 * (g % 2) + t, :], ACT.Copy).then_inc(cT_done, 1)

        @block.vector
        def _(dve):
            for g in range(NGR):
                dve.wait_ge(y_in[g % 2], 16 * (g // 2 + 1))
                dve.wait_ge(a_psum, g + 1)
                y2 = y[g % 2][:].rearrange("p t d -> p (t d)")
                nc.vector.tensor_tensor(y2, ps[:, 4 + 2 * (g % 2):6 + 2 * (g % 2), :].rearrange("p t d -> p (t d)"), y2, ALU.add).then_inc(summed, 1)

        @block.tensor
        def _(pe):
            pe.wait_ge(wo_in, 16)

            def transposes(g):
                if g >= 2:
                    pe.wait_ge(cT_done, (g - 1) * DT)
                for t in range(DT):
                    for i in range(GT):
                        last = nc.tensor.transpose(ps[:, 2 * (g % 2) + t, i * P:(i + 1) * P], ctx_all[:, g * GT + i, t * P:(t + 1) * P], ident[:])
                    last.then_inc(cT_psum, 1)

            transposes(0)
            for g in range(NGR):
                if g + 1 < NGR:
                    transposes(g + 1)
                pe.wait_ge(cT_done, (g + 1) * DT)
                if g >= 2:
                    pe.wait_ge(summed, g - 1)
                for i in range(GT):
                    for t in range(DT):
                        last = nc.tensor.matmul(ps[:, 4 + 2 * (g % 2) + i // 2, (i % 2) * D:(i % 2 + 1) * D], ctxT[g % 2][:, t, i * P:(i + 1) * P], wo_sb[:, t, :],
                                                start=(t == 0), stop=(t == DT - 1))
                last.then_inc(a_psum, 1)


def program(nc, x, wq, wk, wv, wo, bo, w, v, x_cols, wg, wu, b1, b3, wd, a2, b2, out):
    ctx = ExitStack()
    with ctx:
        q_parts = nc.dram_tensor("q_parts", [H + 1, NP, HD, B * N], BF16, kind="Internal").ap()
        k_parts = nc.dram_tensor("k_parts", [H + 1, NP, HD, B * N], BF16, kind="Internal").ap()
        table = nc.dram_tensor("table", [H + 1, TABLE], F32, kind="Internal").ap()
        y_dram = nc.dram_tensor("y_dram", [B, N, D], F32, kind="Internal").ap()
        v_dram = nc.dram_tensor("v_dram", [B, N, D], F32, kind="Internal").ap()
        ident = ctx.enter_context(nc.sbuf_tensor("ident", [P, P], F32))
        ffn_and_projections(nc, x, wq, wk, wv, bo, x_cols, wg, wu, b1, b3, wd, a2, b2, q_parts, k_parts, v_dram, y_dram, ident)
        v_all = ctx.enter_context(nc.sbuf_tensor("v_all", [P, TT, D], F32))
        attention(nc, q_parts, k_parts, v_dram, table, w, v, v_all, ident)
        output_projection(nc, wo, y_dram, v_all, ident, out)


def kernel(**inputs):
    import numpy as np
    import concourse.bacc as bacc
    from concourse.bass_utils import run_bass_kernel_spmd

    a = {n.replace("L0_", ""): np.asarray(t) for n, t in inputs.items()}
    flat = lambda t: t.transpose(2, 0, 1).reshape(t.shape[2], -1)
    er = lambda t: t.transpose(0, 2, 1).reshape(ER, -1)
    arrays = {
        "x": a["attn_x"], "wq": a["attn_Wq"], "wk": a["attn_Wk"], "wv": a["attn_Wv"], "wo": a["attn_Wo"], "bo": a["attn_bo"],
        "w": a["attn_w"], "v": a["attn_v"],
        "x_cols": np.concatenate([flat(a["ffn_A1"]), flat(a["ffn_A3"]), a["ffn_gate_w"].T], axis=1),
        "wg": a["ffn_w_gate"].T, "wu": a["ffn_w_up"].T, "b1": er(a["ffn_B1"]), "b3": er(a["ffn_B3"]),
        "wd": a["ffn_w_down"].T, "a2": flat(a["ffn_A2"]), "b2": er(a["ffn_B2"]),
    }
    arrays = {n: np.ascontiguousarray(t) for n, t in arrays.items()}
    nc = bacc.Bacc("TRN2", target_bir_lowering=False, num_devices=1)
    args = {n: nc.dram_tensor(n, t.shape, F32, kind="ExternalInput").ap() for n, t in arrays.items()}
    out = nc.dram_tensor("out", [B, N, D], F32, kind="ExternalOutput").ap()
    program(nc, out=out, **args)
    return run_bass_kernel_spmd(nc, [arrays], core_ids=[0]).results[0]["out"]
```

```python
import concourse.bass as bass
from concourse import mybir
from contextlib import ExitStack

F32 = mybir.dt.float32
BF16 = mybir.dt.bfloat16
U32 = mybir.dt.uint32
ALU = mybir.AluOpType
ACT = mybir.ActivationFunctionType

P = 128
B, N, D = 4, 2048, 256
H, HD = 16, 16
F, E, R = 1024, 8, 16
ER = E * R
EPS = 1e-5
LORA_SCALE = 2.0
DT = D // P
FT = F // P
G = 512
GT = G // P
GB = N // G
TT = B * N // P
NP = 3
QK_STORES = 2 * DT * NP


PIECES = ["xT0", "xT1", "v0", "v1", "v2", "v3", "u0", "u1", "q0", "q1", "mask0", "mask1", "weight0", "weight1", "k0", "k1"]
NPC = len(PIECES)
JOBS = [(0, 0)] + [job for f in range(1, FT) for job in ((f, 0), (f - 1, 1))] + [(FT - 1, 1)]
NJ = len(JOBS)
JOB_AT = {job: n for n, job in enumerate(JOBS)}
PIECES_AFTER = {1: (0, 1)} | {n: (n,) for n in range(2, NJ)}
NG1 = B * GB


def ffn_and_projections(nc, x, wq, wk, wv_router, bo, a13, wg, wu, b1, b3, wd, a2, b2, q_parts, k_parts, v_dram, y_dram, ident):
    ctx = ExitStack()
    with ctx:
        def sb(name, shape, dt=F32):
            return ctx.enter_context(nc.sbuf_tensor(name, shape, dt))

        def sem(name):
            return ctx.enter_context(nc.semaphore(name))

        wq_sb, wk_sb = (sb(n, [P, DT, D]) for n in ("wq_sb", "wk_sb"))
        wv_router_sb = sb("wv_router_sb", [P, DT, D + E])
        a13_sb = sb("a13_sb", [P, DT, 2 * ER])
        wg_sb, wu_sb = sb("wg_sb", [P, DT, F]), sb("wu_sb", [P, DT, F])
        b1_sb, b3_sb = sb("b1_sb", [P, F]), sb("b3_sb", [P, F])
        wd_sb, a2_sb = sb("wd_sb", [P, FT, D]), sb("a2_sb", [P, FT, ER])
        b2_sb = sb("b2_sb", [P, D])
        bo_sb = sb("bo_sb", [P, D])
        expert_of = sb("expert_of", [P, ER])
        eps_col = sb("eps_col", [P, 1])

        x_sb = sb("x_sb", [P, GT, D])
        bn = sb("bn", [P, GT, 6])
        mean_var = sb("mean_var", [P, GT, 2])
        std, rstd = sb("std", [P, GT]), sb("rstd", [P, GT])
        xn = sb("xn", [P, GT, D])
        qk_f = sb("qk_f", [P, 2, G])
        rest = sb("rest", [P, 2, G])
        parts = sb("parts", [P, 2 * DT, NP, G], BF16)
        v_sb = sb("v_sb", [P, GT, D])
        logits = sb("logits", [P, GT, E])
        top = sb("top", [P, GT, 8])
        top_at = sb("top_at", [P, GT, 8], U32)
        chosen = sb("chosen", [P, GT, 2])
        dlogit, edl, den = sb("dlogit", [P, GT]), sb("edl", [P, GT]), sb("den", [P, GT])
        rw = sb("rw", [P, 2, GT])
        mask = sb("mask", [P, 2, GT, ER])
        weight = sb("weight", [P, 2, GT, P])
        uT = sb("uT", [P, 2, G])
        dmask = sb("dmask", [P, G])
        xnT = [sb(f"xnT{i}", [P, DT, G]) for i in range(2)]
        maskT = [sb(f"maskT{i}", [P, 2, G]) for i in range(2)]
        weightT = [sb(f"weightT{i}", [P, 2, G]) for i in range(2)]
        loraT = [sb(f"loraT{i}", [P, 2, 2, G]) for i in range(2)]
        y_sb = [sb(f"y_sb{i}", [P, GT, D]) for i in range(2)]
        silu, silu_w = sb("silu", [P, 3, G]), sb("silu_w", [P, 3, G])
        act = sb("act", [P, 2, FT, G])
        both = sb("both", [P, FT, G])
        z_a, z_b, zT = sb("z_a", [P, G]), sb("z_b", [P, G]), sb("zT", [P, G])
        ps = ctx.enter_context(nc.psum_tensor("ps", [P, 8, G], F32))

        first_weights_in, weights_in, bo_in, consts, ident_step, scaled = (sem(n) for n in ("first_weights_in", "weights_in", "bo_in", "consts", "ident_step", "scaled"))
        x_in, x_used = sem("x_in"), sem("x_used")
        bn_done, stats_done, std_done, rstd_done, xn_done = (sem(n) for n in ("bn_done", "stats_done", "std_done", "rstd_done", "xn_done"))
        piece_psum, piece_out = sem("piece_psum"), sem("piece_out")
        part1_done, rest_done, part2_done, parts_done, qk_stored = (sem(n) for n in ("part1_done", "rest_done", "part2_done", "parts_done", "qk_stored"))
        v_stored = sem("v_stored")
        top_done, at_done, chosen_done, dl_done, edl_done, den_done, rw0_done, rw_done = (
            sem(n) for n in ("top_done", "at_done", "chosen_done", "dl_done", "edl_done", "den_done", "rw0_done", "rw_done"))
        mask_done, weight_done, dmask_done, lora_done = (sem(n) for n in ("mask_done", "weight_done", "dmask_done", "lora_done"))
        h_psum, silu_done, silu_w_done, act_done, both_done = (sem(n) for n in ("h_psum", "silu_done", "silu_w_done", "act_done", "both_done"))
        z_psum, zm_done, z_done = sem("z_psum"), sem("zm_done"), sem("z_done")
        y_psum, y_done, y_stored = sem("y_psum"), sem("y_done"), sem("y_stored")

        weight_loads = [(dst[:], src.rearrange("(t p) c -> p t c", p=P)) for dst, src in
                        ((a13_sb, a13), (wq_sb, wq), (wk_sb, wk), (wv_router_sb, wv_router), (wg_sb, wg), (wu_sb, wu), (wd_sb, wd), (a2_sb, a2))]
        weight_loads += [(b1_sb[:], b1), (b3_sb[:], b3), (b2_sb[:], b2)]
        FIRST_LOADS = 4
        rows_of = [m.rearrange("b (g t p) d -> (b g) p t d", p=P, t=GT) for m in (x, y_dram, v_dram)]
        x_rows, y_rows, v_rows = rows_of
        block = ctx.enter_context(nc.Block())

        def all_groups(engine, prepare, work):
            prepare(0, 0)
            with engine.Fori(0, NG1 // 2 - 1) as pair:
                for i in range(2):
                    work(2 * pair + i, i, True, True)
            work(NG1 - 2, 0, True, False)
            work(NG1 - 1, 1, False, False)

        @block.sync
        def _(sp):
            def load_x(g):
                sp.dma_start(x_sb[:], x_rows[bass.ds(g, 1)].rearrange("a p t d -> (a p) t d")).then_inc(x_in, 16)

            def store_prepared(g, i):
                for m in range(2 * DT):
                    sp.wait_ge(parts_done, g * (2 * DT) + m + 1)
                    dst = q_parts if m < DT else k_parts
                    heads = slice((m % DT) * H // DT, (m % DT + 1) * H // DT)
                    for a in range(NP):
                        sp.dma_start(dst[heads, a, :, bass.ds(g * G, G)], parts[:, m, a, :]).then_inc(qk_stored, 16)
                sp.wait_ge(piece_out, g * NPC + NPC)
                sp.dma_start(v_rows[bass.ds(g, 1)].rearrange("a p t d -> (a p) t d"), v_sb[:]).then_inc(v_stored, 16)

            def prepare(g, i):
                load_x(0)
                sp.wait_ge(x_used, 1)
                load_x(1)
                store_prepared(g, i)

            def work(g, i, prepares, loads):
                if loads:
                    sp.wait_ge(x_used, g + 2)
                    load_x(g + 2)
                if prepares:
                    store_prepared(g + 1, 1 - i)
                sp.wait_ge(y_done, g * 2 + 4)
                sp.dma_start(y_rows[bass.ds(g, 1)].rearrange("a p t d -> (a p) t d"), y_sb[i][:]).then_inc(y_stored, 16)

            sp.dma_start(bo_sb[:], bo.rearrange("(a n) -> a n", a=1).to_broadcast([P, D])).then_inc(bo_in, 16)
            all_groups(sp, prepare, work)
            sp.wait_ge(qk_stored, 16 * QK_STORES * NG1 + 16)
            sp.wait_ge(v_stored, 16 * NG1 + 16)
            sp.wait_ge(y_stored, 16 * NG1 + 32)

        @block.gpsimd
        def _(pool):
            nc.gpsimd.memset(ident[:], 0.0).then_inc(ident_step, 1)
            pool.wait_ge(ident_step, 1)
            nc.gpsimd.affine_select(out=ident[:], in_=ident[:], compare_op=ALU.not_equal, fill=1.0, base=0,
                                    pattern=[[-1, P]], channel_multiplier=1).then_inc(consts, 1)
            nc.gpsimd.iota(expert_of[:], pattern=[[1, E], [0, R]], base=0, channel_multiplier=0,
                           allow_small_or_imprecise_dtypes=True).then_inc(consts, 1)
            nc.gpsimd.memset(eps_col[:], EPS).then_inc(consts, 1)
            for free, n in ((y_stored, 32), (qk_stored, 16), (v_stored, 16), (y_done, 2), (act_done, NJ), (silu_w_done, NJ), (lora_done, 1), (zm_done, 2)):
                pool.sem_inc(free, n)

            def work(g, i, prepares, loads):
                for n, (f, s) in enumerate(JOBS):
                    pool.wait_ge(act_done, g * NJ + NJ + n - 2)
                    pool.wait_ge(silu_done, g * NJ + n + 1)
                    nc.gpsimd.tensor_tensor(silu_w[:, n % 3, :], silu[:, n % 3, :], weightT[i][:, s, :], ALU.mult).then_inc(silu_w_done, 1)
                    if s == 1 and f >= 1:
                        sum_slots(g, f - 1)
                sum_slots(g, FT - 1)

            def sum_slots(g, f):
                pool.wait_ge(act_done, g * NJ + NJ + JOB_AT[f, 1] + 1)
                pool.wait_ge(y_done, g * 2 + 2)
                nc.gpsimd.tensor_tensor(both[:, f, :], act[:, 0, f, :], act[:, 1, f, :], ALU.add).then_inc(both_done, 1)

            all_groups(pool, lambda g, i: None, work)

        @block.scalar
        def _(act_e):
            for n, (dst, src) in enumerate(weight_loads):
                act_e.dma_start(dst, src).then_inc(first_weights_in if n < FIRST_LOADS else weights_in, 16)
            act_e.wait_ge(consts, 3)
            copy = lambda dst, src: nc.scalar.activation(dst, src, ACT.Copy)

            def std_dev(g):
                act_e.wait_ge(stats_done, g + 1)
                nc.scalar.activation(std[:], mean_var[:, :, 1], ACT.Sqrt, bias=eps_col[:]).then_inc(std_done, 1)

            def piece(g, i, k):
                name = PIECES[k]
                what, t = name[:-1], int(name[-1]) if name[-1].isdigit() else 0
                bank = ps[:, 6 + k % 2, :]
                if name == "q0":
                    act_e.wait_ge(dl_done, g + 1)
                    nc.scalar.activation(edl[:], dlogit[:], ACT.Exp).then_inc(edl_done, 1)
                if name == "v0":
                    act_e.wait_ge(v_stored, g * 16 + 16)
                if what in ("q", "k"):
                    m = t + (DT if what == "k" else 0)
                    if m >= 2:
                        act_e.wait_ge(rest_done, g * (2 * DT) + m - 1)
                if name == "u0":
                    act_e.wait_ge(lora_done, g + 1)
                act_e.wait_ge(piece_psum, g * NPC + k + 1)
                if what == "xT":
                    last = copy(xnT[i][:, t, :], bank)
                elif what == "u":
                    last = copy(uT[:, t, :], bank)
                elif what in ("q", "k"):
                    last = copy(qk_f[:, m % 2, :], bank)
                elif what == "mask":
                    last = copy(maskT[i][:, t, :], bank)
                elif what == "weight":
                    last = copy(weightT[i][:, t, :], bank)
                else:
                    copy(logits[:, t, :], bank[:, D:D + E])
                    last = copy(v_sb[:, t, :], bank[:, 0:D])
                last.then_inc(piece_out, 1)

            def prepare(g, i):
                std_dev(g)
                for k in range(NPC):
                    piece(g, i, k)

            def work(g, i, prepares, loads):
                if prepares:
                    std_dev(g + 1)
                for n, (f, s) in enumerate(JOBS):
                    act_e.wait_ge(silu_w_done, g * NJ + NJ + n - 2)
                    act_e.wait_ge(h_psum, g * NJ + n + 1)
                    nc.scalar.activation(silu[:, n % 3, :], ps[:, 2 * (f % 3), :], ACT.Silu).then_inc(silu_done, 1)
                    for k in PIECES_AFTER.get(n, ()) if prepares else ():
                        piece(g + 1, 1 - i, k)

            all_groups(act_e, prepare, work)

        @block.vector
        def _(dve):
            dve.wait_ge(bo_in, 16)
            dve.wait_ge(consts, 3)

            def layer_norm(g, i):
                dve.wait_ge(x_in, g * 16 + 16)
                for t in range(GT):
                    nc.vector.bn_stats(bn[:, t, :], x_sb[:, t, :]).then_inc(bn_done, 1)
                dve.wait_ge(bn_done, g * GT + GT)
                nc.vector.memset(rstd[:], 0.0)
                for t in range(GT):
                    last = nc.vector.bn_aggr(mean_var[:, t, :], bn[:, t, :])
                last.then_inc(stats_done, 1)
                dve.wait_ge(std_done, g + 1)
                nc.vector.reciprocal(rstd[:], std[:]).then_inc(rstd_done, 1)
                dve.wait_ge(rstd_done, g + 1)
                for t in range(GT):
                    last = nc.vector.tensor_scalar(xn[:, t, :], x_sb[:, t, :], mean_var[:, t, 0:1], rstd[:, t:t + 1], ALU.subtract, ALU.mult)
                last.then_inc(xn_done, 1)

            def start_y(g, i):
                dve.wait_ge(y_stored, g * 16 + 16)
                nc.vector.tensor_tensor(y_sb[i][:], x_sb[:], bo_sb[:].unsqueeze(1).to_broadcast([P, GT, D]), ALU.add).then_inc(x_used, 1)

            def split(g, m, out):
                if m == 0:
                    dve.wait_ge(qk_stored, g * (16 * QK_STORES) + 16)
                dve.wait_ge(piece_out, g * NPC + out + 1)
                nc.vector.tensor_copy(parts[:, m, 0, :], qk_f[:, m % 2, :]).then_inc(part1_done, 1)
                dve.wait_ge(part1_done, g * (2 * DT) + m + 1)
                nc.vector.tensor_tensor(rest[:, m % 2, :], qk_f[:, m % 2, :], parts[:, m, 0, :], ALU.subtract).then_inc(rest_done, 1)
                dve.wait_ge(rest_done, g * (2 * DT) + m + 1)
                nc.vector.tensor_copy(parts[:, m, 1, :], rest[:, m % 2, :]).then_inc(part2_done, 1)
                dve.wait_ge(part2_done, g * (2 * DT) + m + 1)
                nc.vector.tensor_tensor(parts[:, m, 2, :], rest[:, m % 2, :], parts[:, m, 1, :], ALU.subtract).then_inc(parts_done, 1)

            def experts(g):
                for t in range(GT):
                    nc.vector.max(top[:, t, :], logits[:, t, :]).then_inc(top_done, 1)
                dve.wait_ge(top_done, g * GT + GT)
                nc.vector.tensor_tensor(dlogit[:], top[:, :, 1], top[:, :, 0], ALU.subtract).then_inc(dl_done, 1)
                for t in range(GT):
                    last = nc.vector.max_index(top_at[:, t, :], top[:, t, :], logits[:, t, :])
                last.then_inc(at_done, 1)
                dve.wait_ge(at_done, g + 1)
                nc.vector.tensor_copy(chosen[:], top_at[:, :, 0:2]).then_inc(chosen_done, 1)

            def masks(g):
                dve.wait_ge(chosen_done, g + 1)
                for s in range(2):
                    for t in range(GT):
                        last = nc.vector.tensor_scalar(mask[:, s, t, :], expert_of[:], chosen[:, t, s:s + 1], None, ALU.is_equal)
                last.then_inc(mask_done, 1)

            def weights(g):
                dve.wait_ge(edl_done, g + 1)
                nc.vector.tensor_scalar(den[:], edl[:], 1.0, None, ALU.add).then_inc(den_done, 1)
                dve.wait_ge(den_done, g + 1)
                nc.vector.reciprocal(rw[:, 0, :], den[:]).then_inc(rw0_done, 1)
                dve.wait_ge(rw0_done, g + 1)
                nc.vector.tensor_tensor(rw[:, 1, :], edl[:], rw[:, 0, :], ALU.mult).then_inc(rw_done, 1)
                dve.wait_ge(rw_done, g + 1)
                nc.vector.tensor_copy(weight[:].rearrange("p s t c -> p (s t) c"),
                                      rw[:].rearrange("p s t -> p (s t)").unsqueeze(2).to_broadcast([P, 2 * GT, P])).then_inc(weight_done, 1)

            def masked(g, i):
                dve.wait_ge(piece_out, g * NPC + PIECES.index("mask1") + 1)
                nc.vector.tensor_tensor(dmask[:], maskT[i][:, 1, :], maskT[i][:, 0, :], ALU.subtract).then_inc(dmask_done, 1)
                for a in range(2):
                    nc.vector.tensor_tensor(loraT[i][:, 0, a, :], uT[:, a, :], maskT[i][:, 0, :], ALU.mult)
                dve.wait_ge(dmask_done, g + 1)
                for a in range(2):
                    last = nc.vector.tensor_tensor(loraT[i][:, 1, a, :], uT[:, a, :], dmask[:], ALU.mult)
                last.then_inc(lora_done, 1)

            EXPERTS_AT = 7
            steps = {3: (start_y,), EXPERTS_AT: (lambda g, i: experts(g),), 8: (lambda g, i: masks(g),),
                     9: (lambda g, i: split(g, 0, PIECES.index("q0")),), 10: (lambda g, i: weights(g),),
                     11: (lambda g, i: split(g, 1, PIECES.index("q1")),), 13: (masked,),
                     15: (lambda g, i: split(g, 2, PIECES.index("k0")), lambda g, i: split(g, 3, PIECES.index("k1")))}

            def prepare(g, i):
                layer_norm(g, i)
                for n in sorted(steps):
                    if n == EXPERTS_AT:
                        dve.wait_ge(piece_out, g * NPC + PIECES.index("v3") + 1)
                        nc.vector.memset(den[:], 0.0)
                    for step in steps[n]:
                        step(g, i)
                dve.wait_ge(weights_in, 16 * (len(weight_loads) - FIRST_LOADS))
                for w in (b1_sb, b3_sb, b2_sb):
                    nc.vector.tensor_scalar(w[:], w[:], LORA_SCALE, None, ALU.mult).then_inc(scaled, 1)

            def work(g, i, prepares, loads):
                if prepares:
                    layer_norm(g + 1, 1 - i)
                for n, (f, s) in enumerate(JOBS):
                    if prepares and n == EXPERTS_AT:
                        dve.wait_ge(piece_out, (g + 1) * NPC + PIECES.index("v3") + 1)
                    dve.wait_ge(silu_w_done, g * NJ + NJ + n + 1)
                    nc.vector.tensor_tensor(act[:, s, f, :], ps[:, 2 * (f % 3) + 1, :], silu_w[:, n % 3, :], ALU.mult).then_inc(act_done, 1)
                    for step in steps.get(n, ()) if prepares else ():
                        step(g + 1, 1 - i)
                for s, z in enumerate((z_a, z_b)):
                    dve.wait_ge(z_psum, g * 2 + s + 1)
                    nc.vector.tensor_tensor(z[:], ps[:, 4 + s, :], maskT[i][:, s, :], ALU.mult).then_inc(zm_done, 1)
                dve.wait_ge(zm_done, g * 2 + 4)
                nc.vector.tensor_tensor(zT[:], z_a[:], z_b[:], ALU.add).then_inc(z_done, 1)
                for k in range(2):
                    dve.wait_ge(y_psum, g * 2 + k + 1)
                    y = y_sb[i][:, 2 * k:2 * k + 2, :].rearrange("p t d -> p (t d)")
                    nc.vector.tensor_tensor(y, ps[:, 6 + k, :], y, ALU.add).then_inc(y_done, 1)

            all_groups(dve, prepare, work)

        @block.tensor
        def _(pe):
            mm = nc.tensor.matmul
            pe.wait_ge(first_weights_in, 16 * FIRST_LOADS)
            pe.wait_ge(consts, 3)

            def piece(g, i, k, first=False):
                name = PIECES[k]
                what, t = name[:-1], int(name[-1]) if name[-1].isdigit() else 0
                bank = ps[:, 6 + k % 2, :]
                if k < 2 and not first:
                    pe.wait_ge(y_done, g * 2 + k - 1)
                elif k >= 2:
                    pe.wait_ge(piece_out, g * NPC + k - 1)
                if what == "xT":
                    pe.wait_ge(xn_done, g + 1)
                    for n in range(GT):
                        last = nc.tensor.transpose(bank[:, n * P:(n + 1) * P], xn[:, n, t * P:(t + 1) * P], ident[:])
                elif what in ("u", "q", "k"):
                    w = {"u": a13_sb, "q": wq_sb, "k": wk_sb}[what]
                    for d in range(DT):
                        last = mm(bank, w[:, d, t * P:(t + 1) * P], xnT[i][:, d, :], start=(d == 0), stop=(d == DT - 1))
                elif what in ("mask", "weight"):
                    pe.wait_ge(mask_done if what == "mask" else weight_done, g + 1)
                    src = mask if what == "mask" else weight
                    for n in range(GT):
                        last = nc.tensor.transpose(bank[:, n * P:(n + 1) * P], src[:, t, n, :], ident[:])
                else:
                    if t == 0:
                        pe.wait_ge(piece_out, g * NPC + PIECES.index("xT1") + 1)
                    for d in range(DT):
                        last = mm(bank[:, 0:D + E], xnT[i][:, d, t * P:(t + 1) * P], wv_router_sb[:, d, :], start=(d == 0), stop=(d == DT - 1))
                last.then_inc(piece_psum, 1)

            def prepare(g, i):
                for k in range(NPC):
                    piece(g, i, k, first=True)
                pe.wait_ge(weights_in, 16 * (len(weight_loads) - FIRST_LOADS))
                pe.wait_ge(scaled, 3)

            def work(g, i, prepares, loads):
                pe.wait_ge(lora_done, g + 2)
                for n, (f, s) in enumerate(JOBS):
                    gate, up = ps[:, 2 * (f % 3), :], ps[:, 2 * (f % 3) + 1, :]
                    cols = slice(f * P, (f + 1) * P)
                    if s == 0:
                        if f >= 3:
                            pe.wait_ge(act_done, g * NJ + NJ + JOB_AT[f - 3, 1] + 1)
                        else:
                            pe.wait_ge(act_done, g * NJ + NJ)
                            if f == 2:
                                pe.wait_ge(zm_done, g * 2 + 2)
                        for w, b, out, a in ((wg_sb, b1_sb, gate, 0), (wu_sb, b3_sb, up, 1)):
                            for d in range(DT):
                                mm(out, w[:, d, cols], xnT[i][:, d, :], start=(d == 0), stop=False)
                            last = mm(out, b[:, cols], loraT[i][:, 0, a, :], start=False, stop=True)
                    else:
                        pe.wait_ge(act_done, g * NJ + NJ + JOB_AT[f, 0] + 1)
                        for b, out, a in ((b1_sb, gate, 0), (b3_sb, up, 1)):
                            last = mm(out, b[:, cols], loraT[i][:, 1, a, :], start=False, stop=True, skip_group_check=True)
                    last.then_inc(h_psum, 1)
                    for k in PIECES_AFTER.get(n, ()) if prepares else ():
                        piece(g + 1, 1 - i, k)
                pe.wait_ge(act_done, g * NJ + NJ + JOB_AT[FT - 3, 1] + 1)
                for s in range(2):
                    for f in range(FT):
                        if f >= FT - 2:
                            pe.wait_ge(act_done, g * NJ + NJ + JOB_AT[f, s] + 1)
                        last = mm(ps[:, 4 + s, :], a2_sb[:, f, :], act[:, s, f, :], start=(f == 0), stop=(f == FT - 1))
                    last.then_inc(z_psum, 1)
                if prepares:
                    pe.wait_ge(piece_out, (g + 1) * NPC + NPC)
                pe.wait_ge(both_done, g * FT + FT)
                for n in range(GT):
                    out, tile = ps[:, 6 + n // 2, (n % 2) * D:(n % 2 + 1) * D], slice(n * P, (n + 1) * P)
                    for f in range(FT):
                        mm(out, both[:, f, tile], wd_sb[:, f, :], start=(f == 0), stop=False)
                    if n == 0:
                        pe.wait_ge(z_done, g + 1)
                    last = mm(out, zT[:, tile], b2_sb[:], start=False, stop=True)
                    if n % 2:
                        last.then_inc(y_psum, 1)

            all_groups(pe, prepare, work)


QT = N // P
SLOT = 1024
CHUNK = 512
CB = CHUNK // P // 2
QW = 32
ROWS = 8 * HD
MASKED = -1e30
SM_SCALE = 1.0 / HD ** 0.5
TABLE = P - 1 + N
OG = G // P


def attention(nc, q_parts, k_parts, v_dram, table, w, v, v_all, ident):
    ctx = ExitStack()
    with ctx:
        def sb(name, shape, dt=F32):
            return ctx.enter_context(nc.sbuf_tensor(name, shape, dt))

        def sem(name):
            return ctx.enter_context(nc.semaphore(name))

        DC = N // P
        zero = sb("zero", [P, P])
        factor = sb("factor", [P, N])
        factor_next = sb("factor_next", [P, N])
        NROW = 8
        hide = sb("hide", [P, P])
        w_neg, v_bc, ev1 = sb("w_neg", [P, H]), sb("v_bc", [P, H]), sb("ev1", [P, H])
        qx = [sb(f"qx{j}", [P, N], BF16) for j in range(B)]
        kx = [sb(f"kx{j}", [P, N], BF16) for j in range(B)]
        vx = [sb(f"vx{j}", [P, QT, QW]) for j in range(B)]
        none = sb("none", [P, P], BF16)
        rows = [sb(f"rows{i}", [P, N]) for i in range(NROW)]
        factors = rows[0][:, 0:H * DC].rearrange("p (h c) -> p h c", h=H)
        dist = rows[1][:, 0:DC]
        top = sb("row_max", [P, 8])
        unused = sb("unused", [P, 8])
        probs = [sb(f"probs{i}", [P, CHUNK]) for i in range(4)]
        o_parts = [sb(f"o_parts{i}", [P, G]) for i in range(2)]
        fold = sb("fold", [P, 2 * QW])
        inv = sb("inv", [P, 2, 2 * OG])
        ps = ctx.enter_context(nc.psum_tensor("ps_attn", [P, 8, G], F32))

        dist_done, zero_done, const_step, consts, wv_in, wv_done, ev_done = (sem(n) for n in ("dist_done", "zero_done", "const_step", "a_consts", "wv_in", "wv_done", "ev_done"))
        decay_done, factor_step, table_stored = sem("decay_done"), sem("factor_step"), sem("table_stored")
        factor_in, factor_taken, spare_stored = sem("factor_in"), sem("factor_taken"), sem("spare_stored")
        qk_in = [sem(f"qk_in{j}") for j in range(B)]
        v_in = [sem(f"v_in{j}") for j in range(B)]
        vx_done = sem("vx_done")
        s_psum, scaled = sem("s_psum"), sem("s_scaled")
        row_done, diag_done = sem("row_done"), sem("diag_done")
        t_psum, probs_done = sem("t_psum"), sem("probs_done")
        pv_done = sem("pv_done")
        o_done, f_psum = sem("o_done"), sem("f_psum")
        inv_done, normed = sem("inv_done"), sem("normed")

        tiles = [(j, t) for b in range(0, B, 2) for i in range(0, QT, 2) for j, last in ((b, QT - 1 - i), (b + 1, i + 1)) for t in (last, last - 1)]
        slots, chunks = [], []
        for n, (j, t) in enumerate(tiles):
            keys = (t + 1) * P
            slots += [(n, k, min(SLOT, keys - k)) for k in range(0, keys, SLOT)]
            if n % 2 == 0:
                chunks += [(n // 2, kb, CB + min(CB, t - kb)) for kb in range(0, t + 1, CB)]
        NT, NS, NC, NG = len(tiles), len(slots), len(chunks), len(tiles) // 2 // OG
        assert NS % 2 == 0 and NC % 4 == 0 and NT % 2 == 0 and NG % 2 == 0
        slots_of = [[c for c, s in enumerate(slots) if s[0] == n] for n in range(NT)]
        last_chunk = [max(c for c, s in enumerate(chunks) if s[0] == n // 2) for n in range(NT)]
        last_of_group = [last_chunk[2 * OG * (g + 1) - 1] for g in range(NG)]
        last_of = [max(n for n in range(NT) if tiles[n][0] == j) for j in range(B)]
        first_of = [min(n for n in range(NT) if tiles[n][0] == j) for j in range(B)]
        tile_of = lambda c: c // NS * NT + slots[c % NS][0]
        ends_tile = lambda c: tile_of(c + 1) != tile_of(c)
        end_slot = lambda n: n // NT * NS + slots_of[n % NT][-1]
        first_key_block = lambda c: c // NS * sum(kn for _, _, kn in slots) // P + sum(kn for _, _, kn in slots[:c % NS]) // P
        LAG_O, LAG_F = 3, 5
        LAG_P = 2
        evac_after = {min(last_of_group[g] + LAG_O, NC - 1): g for g in range(NG)}
        fold_after = {min(last_of_group[g] + LAG_F, NC - 1): g for g in range(NG)}
        LEAD = 42
        TAIL = 2
        AHEAD = next(c for c in range(NS) if first_key_block(c) > LEAD)
        slots_after, made, t_blocks = [[] for _ in range(NC + 1)], AHEAD, 0
        norm_before = {}
        for k in range(NC + 1):
            tile = 2 * chunks[k][0] if k < NC else NT
            while made < NS + AHEAD - TAIL and (made <= end_slot(tile + 1) + 1 or k == NC
                                                or first_key_block(made) <= t_blocks + LEAD and tile_of(made - 2) - NROW < tile):
                slots_after[k].append(made)
                made += 1
            t_blocks += chunks[k][2] if k < NC else 0
            g = fold_after.get(k - 1 - LAG_P)
            if g is not None and g < NG - 1:
                norm_before.setdefault(min(max(made, end_slot(2 * chunks[k - 1][0] + 1) + 2), NS + AHEAD), []).append(g)
        norm_before.setdefault(NS + AHEAD, []).append(NG - 1)
        LOADS = 5
        credits = [(s_psum, NS), (scaled, 2), (t_psum, NC), (probs_done, 2), (pv_done, NC), (f_psum, 2), (normed, 2)]
        assert len(probs) == 4

        block = ctx.enter_context(nc.Block())

        @block.sync
        def _(sp):
            sp.dma_start(w_neg[:], w.rearrange("(a n) -> a n", a=1).to_broadcast([P, H])).then_inc(wv_in, 16)
            sp.dma_start(v_bc[:], v.rearrange("(a n) -> a n", a=1).to_broadcast([P, H])).then_inc(wv_in, 16)

            def load_factor(h):
                sp.dma_start(factor_next[:], bass.AP(tensor=table.tensor, offset=h * TABLE, ap=[[1, P], [1, N]])).then_inc(factor_in, 16)

            def load_qk(h, j):
                q = q_parts[bass.ds(h, 1), :, :, j * N:(j + 1) * N].rearrange("h a d t -> (h a d) t")
                k = k_parts[bass.ds(h, 1), :, :, j * N:(j + 1) * N].rearrange("h a d t -> (h a) d t")
                sp.dma_start(qx[j][0:2 * NP * HD, :], q.unsqueeze(0).to_broadcast([2, NP * HD, N])).then_inc(qk_in[j], 16)
                sp.dma_start(qx[j][2 * NP * HD:ROWS, :], q[0:2 * HD, :]).then_inc(qk_in[j], 16)
                for a, (r0, r1) in enumerate(((0, 3), (3, 6), (6, 8))):
                    sp.dma_start(kx[j][r0 * HD:r1 * HD, :], k[a:a + 1].to_broadcast([r1 - r0, HD, N])).then_inc(qk_in[j], 16)

            load_qk(0, 0)
            sp.wait_ge(factor_step, 3)
            for dst, src in [(table[0:H, P - 1:TABLE], factors), (table[H:H + 1, P - 1:TABLE], factors[:, 0:1, :])]:
                sp.dma_start(dst.rearrange("h (p c) -> p h c", p=P), src).then_inc(table_stored, 16)
            sp.wait_ge(zero_done, 1)
            sp.dma_start(table[:, 0:P - 1], zero[0:H + 1, 0:P - 1]).then_inc(table_stored, 16)
            load_qk(0, 1)
            sp.wait_ge(table_stored, 48)
            load_factor(0)
            for j in range(B):
                if j >= 2:
                    load_qk(0, j)
                sp.dma_start(v_all[:, j * QT:(j + 1) * QT, :], v_dram[j].rearrange("(t p) d -> p t d", p=P)).then_inc(v_in[j], 16)
            for m in (q_parts, k_parts):
                sp.dma_start(m[H].rearrange("a d t -> (a d) t"), m[0].rearrange("a d t -> (a d) t")).then_inc(spare_stored, 16)
            sp.wait_ge(spare_stored, 32)
            with sp.Fori(0, H) as h:
                sp.wait_ge(factor_taken, h + 1)
                load_factor(h + 1)
                for j in range(B):
                    sp.wait_ge(s_psum, h * NS + NS + slots_of[last_of[j]][-1] + 1)
                    load_qk(h + 1, j)
            for j in range(B):
                sp.wait_ge(qk_in[j], 16 * LOADS * (H + 1))
            sp.wait_ge(factor_in, 16 * (H + 1))

        @block.gpsimd
        def _(pool):
            nc.gpsimd.iota(dist, pattern=[[1, DC]], base=0, channel_multiplier=DC, allow_small_or_imprecise_dtypes=True).then_inc(dist_done, 1)
            nc.gpsimd.memset(zero[:], 0.0).then_inc(zero_done, 1)
            nc.gpsimd.memset(hide[:], 0.0).then_inc(const_step, 1)
            nc.gpsimd.memset(fold[:], 0.0).then_inc(const_step, 1)
            nc.gpsimd.memset(none[:], 0.0).then_inc(consts, 1)
            for j in range(B):
                nc.gpsimd.memset(vx[j][:], 0.0).then_inc(const_step, 1)
            pool.wait_ge(const_step, 2 + B)
            for j in range(B):
                nc.gpsimd.memset(vx[j][:, :, HD:HD + 1], 1.0).then_inc(consts, 1)
            nc.gpsimd.affine_select(out=hide[:], in_=hide[:], compare_op=ALU.is_ge, fill=MASKED, base=0,
                                    pattern=[[-1, P]], channel_multiplier=1).then_inc(consts, 1)
            for i in range(2 * CB):
                half = fold[:, i // CB * QW:(i // CB + 1) * QW]
                nc.gpsimd.affine_select(out=half, in_=half, compare_op=ALU.not_equal, fill=1.0, base=-QW * i,
                                        pattern=[[-1, QW]], channel_multiplier=1).then_inc(const_step, 1)
                pool.wait_ge(const_step, 3 + B + i)
            for free, n in credits:
                pool.sem_inc(free, n)
            pool.wait_ge(consts, 2 + B)
            pool.sem_inc(consts, 1)
            with pool.Fori(0, H) as h:
                for n, (j, t) in enumerate(tiles):
                    if n == first_of[j]:
                        pool.wait_ge(v_in[j], 16)
                        pool.wait_ge(pv_done, h * NC + last_chunk[last_of[j]] + 1)
                    pool.wait_ge(row_done, h * NT + n + 1)
                    diag = rows[n % NROW][:, t * P:(t + 1) * P]
                    nc.gpsimd.tensor_tensor(diag, diag, hide[:], ALU.add).then_inc(diag_done, 1)
                    if n == first_of[j]:
                        nc.gpsimd.tensor_copy(vx[j][:, :, 0:HD], v_all[:, bass.ds(j * QT, QT), bass.ds(h * HD, HD)]).then_inc(vx_done, 1)

        @block.scalar
        def _(act_e):
            act_e.wait_ge(wv_in, 32)
            nc.scalar.activation(ev1[:], v_bc[:], ACT.Exp).then_inc(ev_done, 1)
            act_e.wait_ge(wv_done, 2)
            act_e.wait_ge(dist_done, 1)
            for h in range(H):
                nc.scalar.activation(factors[:, h, :], dist, ACT.Exp, scale=w_neg[:, h:h + 1], bias=v_bc[:, h:h + 1]).then_inc(decay_done, 1)
            with act_e.Fori(0, H) as h:
                for c, (n, kb, m) in enumerate(chunks):
                    act_e.wait_ge(pv_done, h * NC + NC + c - 3)
                    act_e.wait_ge(t_psum, h * NC + NC + c + 1)
                    nc.scalar.activation(probs[c % 4][:, 0:m * P], ps[:, 4 + c % 2, 0:m * P], ACT.Exp, scale=SM_SCALE).then_inc(probs_done, 1)
                    if c in evac_after:
                        g = evac_after[c]
                        act_e.wait_ge(f_psum, h * NG + g + 1)
                        act_e.wait_ge(pv_done, h * NC + NC + last_of_group[g] + 1)
                        nc.scalar.activation(o_parts[g % 2][:], ps[:, 6 + g % 2, :], ACT.Copy).then_inc(o_done, 1)

        @block.vector
        def _(dve):
            dve.wait_ge(wv_in, 32)
            nc.vector.tensor_scalar(w_neg[:], w_neg[:], -1.0, None, ALU.mult).then_inc(wv_done, 1)
            dve.wait_ge(ev_done, 1)
            nc.vector.tensor_scalar(ev1[:], ev1[:], 1.0, None, ALU.add).then_inc(wv_done, 1)
            dve.wait_ge(wv_done, 2)
            dve.wait_ge(decay_done, H)
            nc.vector.tensor_scalar(factors, factors, 1.0, None, ALU.add).then_inc(factor_step, 1)
            dve.wait_ge(factor_step, 1)
            nc.vector.reciprocal(factors, factors).then_inc(factor_step, 1)
            dve.wait_ge(factor_step, 2)
            nc.vector.tensor_tensor(factors, factors, ev1[:].unsqueeze(2).to_broadcast([P, H, DC]), ALU.mult).then_inc(factor_step, 1)

            def take_factor(h):
                dve.wait_ge(factor_in, h * 16 + 16)
                dve.wait_ge(scaled, h * NS + 2)
                nc.vector.tensor_copy(factor[:], factor_next[:]).then_inc(factor_taken, 1)

            def invert(h, g):
                dve.wait_ge(f_psum, h * NG + g + 3)
                nc.vector.reciprocal(inv[:, g % 2, :], ps[:, 6 + g % 2, 0:2 * OG * QW].rearrange("p (t c) -> p t c", c=QW)[:, :, HD]).then_inc(inv_done, 1)

            def normalise(h, g):
                o = ps[:, 6 + g % 2, 0:2 * OG * QW].rearrange("p (t c) -> p t c", c=QW)
                dve.wait_ge(inv_done, h * NG + g + 1)
                for p in range(OG):
                    order = slice(2 * p + 1, 2 * p - 1 if p else None, -1)
                    j, t = tiles[2 * (OG * g + p) + 1]
                    ins = nc.vector.tensor_tensor(v_all[:, bass.ds(j * QT + t, 2), bass.ds(h * HD, HD)], o[:, order, 0:HD],
                                                  inv[:, g % 2, order].unsqueeze(2).to_broadcast([P, 2, HD]), ALU.mult)
                ins.then_inc(normed, 1)

            def less_max(h, n, c):
                t = tiles[n % NT][1]
                row = rows[n % NROW][:, 0:(t + 1) * P]
                dve.wait_ge(scaled, h * NS + c + 3)
                nc.vector.tensor_scalar(row, row, 0.0, top[:, c % 8:c % 8 + 1], ALU.max, ALU.subtract).then_inc(row_done, 1)

            def scale(h, c):
                n, k0, kn = tile_of(c), slots[c % NS][1], slots[c % NS][2]
                if c % NS == 0:
                    take_factor(h + c // NS)
                dve.wait_ge(s_psum, h * NS + NS + c + 1)
                if k0:
                    dve.wait_ge(scaled, h * NS + c + 2)
                else:
                    old = n - NROW + NT
                    dve.wait_ge(t_psum, h * NC + old // NT * NC + last_chunk[old % NT] + 1)
                if c % NS == 0:
                    dve.wait_ge(factor_taken, h + c // NS + 1)
                nc.vector.memset(unused[:, c % 8:c % 8 + 1], 0.0)
                at_k0 = tiles[n % NT][1] * P + P - 1 - k0
                row = factor[:, at_k0::-1] if at_k0 == kn - 1 else factor[:, at_k0:at_k0 - kn:-1]
                so_far = top[:, (c - 1) % 8:(c - 1) % 8 + 1] if k0 else 0.0
                nc.vector.tensor_tensor_reduce(out=rows[n % NROW][:, k0:k0 + kn], in0=ps[:, 2 * (c % 2):2 * (c % 2) + 2, :].rearrange("p a b -> p (a b)")[:, 0:kn],
                                               in1=row, scale=1.0, scalar=so_far,
                                               op0=ALU.mult, op1=ALU.max, accum_out=top[:, c % 8:c % 8 + 1]).then_inc(scaled, 1)

            def tile_behind(h, c):
                if c > 0 and ends_tile(c - 1):
                    less_max(h, tile_of(c - 1), c - 1)

            for c in range(AHEAD):
                scale(0, c)
                tile_behind(0, c)
            with dve.Fori(0, H) as h:
                for c in range(AHEAD, NS + AHEAD):
                    for g in norm_before.get(c, []):
                        invert(h, g)
                    scale(h, c)
                    for g in norm_before.get(c, []):
                        normalise(h, g)
                    tile_behind(h, c)
                for g in norm_before[NS + AHEAD]:
                    invert(h, g)
                    normalise(h, g)

        @block.tensor
        def _(pe):
            mm = nc.tensor.matmul
            pe.wait_ge(consts, 3 + B)

            def scores(h, c):
                h, c = (h + 1, c - NS) if c >= NS else (h, c)
                n, k0, kn = slots[c]
                j, t = tiles[n]
                if n == first_of[j] and k0 == 0:
                    pe.wait_ge(qk_in[j], h * (16 * LOADS) + 16 * LOADS)
                pe.wait_ge(scaled, h * NS + c + 1)
                for i, k in enumerate(range(0, kn, G)):
                    wd = min(G, kn - k)
                    last = mm(ps[:, 2 * (c % 2) + i, 0:wd], qx[j][:, t * P:(t + 1) * P], kx[j][:, k0 + k:k0 + k + wd], start=True, stop=True)
                last.then_inc(s_psum, 1)

            for c in range(AHEAD):
                scores(0, c)
            with pe.Fori(0, H) as h:
                def transposed(c):
                    pair, kb, m = chunks[c]
                    pe.wait_ge(row_done, h * NT + 2 * pair + 2)
                    if c == last_chunk[2 * pair]:
                        pe.wait_ge(diag_done, h * NT + 2 * pair + 2)
                    pe.wait_ge(probs_done, h * NC + c + 1)
                    for i in range(m):
                        n, k = 2 * pair + i // CB, kb + i % CB
                        last = nc.tensor.transpose(ps[:, 4 + c % 2, i * P:(i + 1) * P], rows[n % NROW][:, k * P:(k + 1) * P], ident[:])
                    last.then_inc(t_psum, 1)

                def output(c):
                    pair, kb, m = chunks[c]
                    j = tiles[2 * pair][0]
                    g = pair // OG
                    if kb == 0 and 2 * pair == first_of[j]:
                        pe.wait_ge(vx_done, h * B + j + 1)
                    if kb == 0 and pair % OG == 0:
                        pe.wait_ge(normed, h * NG + g + 1)
                    pe.wait_ge(probs_done, h * NC + c + 3)
                    cols = slice((pair % OG) * P, (pair % OG + 1) * P)
                    for i in range(2 * CB):
                        t, k = tiles[2 * pair + i // CB][1], kb + i % CB
                        o = ps[i * QW:(i + 1) * QW, 6 + g % 2, cols]
                        if i < m:
                            last = mm(o, vx[j][:, k, :], probs[c % 4][:, i * P:(i + 1) * P], start=(kb == 0), stop=(k + CB > t))
                        elif kb == 0:
                            last = mm(o, none[:, 0:QW], none[:], start=True, stop=True)
                    last.then_inc(pv_done, 1)

                def folded(g):
                    pe.wait_ge(o_done, h * NG + g + 1)
                    for i in range(OG):
                        last = mm(ps[:, 6 + g % 2, 2 * i * QW:2 * (i + 1) * QW], o_parts[g % 2][:, i * P:(i + 1) * P], fold[:], start=True, stop=True)
                    last.then_inc(f_psum, 1)

                for c in slots_after[0]:
                    scores(h, c)
                for c in range(NC):
                    transposed(c)
                    for s in slots_after[c + 1]:
                        scores(h, s)
                    if c >= LAG_P:
                        output(c - LAG_P)
                        if c - LAG_P in fold_after:
                            folded(fold_after[c - LAG_P])
                for c in range(NC - LAG_P, NC):
                    output(c)
                    for s in range(NS + AHEAD - TAIL, NS + AHEAD)[c - (NC - LAG_P)::LAG_P]:
                        scores(h, s)
                folded(NG - 1)


def output_projection(nc, wo, y_dram, ctx_all, ident, out):
    ctx = ExitStack()
    with ctx:
        def sb(name, shape, dt=F32):
            return ctx.enter_context(nc.sbuf_tensor(name, shape, dt))

        def sem(name):
            return ctx.enter_context(nc.semaphore(name))

        wo_sb = sb("wo_sb", [P, DT, D])
        y = [sb(f"y{i}", [P, GT, D]) for i in range(2)]
        ctxT = [sb(f"ctxT{i}", [P, DT, G]) for i in range(2)]
        ps = ctx.enter_context(nc.psum_tensor("ps_out", [P, 8, G], F32))
        wo_in, copied = sem("wo_in"), sem("copied")
        y_in = [sem(f"y_in{i}") for i in range(2)]
        stored = [sem(f"stored{i}") for i in range(2)]
        cT_psum, cT_done, a_psum, summed = sem("cT_psum"), sem("cT_done"), sem("a_psum"), sem("summed")
        NGR = B * GB
        y_rows = y_dram.rearrange("b (g t p) d -> (b g) p t d", p=P, t=GT)
        out_rows = out.rearrange("b (g t p) d -> (b g) p t d", p=P, t=GT)
        block = ctx.enter_context(nc.Block())

        @block.sync
        def _(sp):
            sp.dma_start(wo_sb[:], wo.rearrange("(t p) c -> p t c", p=P)).then_inc(wo_in, 16)
            for g in range(2):
                sp.dma_start(y[g][:], y_rows[g]).then_inc(y_in[g], 16)
            for g in range(NGR):
                sp.wait_ge(summed, g + 1)
                sp.dma_start(out_rows[g], y[g % 2][:]).then_inc(stored[g % 2], 16)
                if g + 2 < NGR:
                    sp.wait_ge(stored[g % 2], 16 * (g // 2 + 1))
                    sp.dma_start(y[g % 2][:], y_rows[g + 2]).then_inc(y_in[g % 2], 16)
            for i in range(2):
                sp.wait_ge(stored[i], 16 * (NGR // 2))

        @block.scalar
        def _(act_e):
            for g in range(NGR):
                if g >= 2:
                    act_e.wait_ge(a_psum, g - 1)
                for t in range(DT):
                    act_e.wait_ge(cT_psum, g * DT + t + 1)
                    nc.scalar.activation(ctxT[g % 2][:, t, :], ps[:, 2 * (g % 2) + t, :], ACT.Copy).then_inc(cT_done, 1)

        @block.vector
        def _(dve):
            for g in range(NGR):
                dve.wait_ge(y_in[g % 2], 16 * (g // 2 + 1))
                dve.wait_ge(a_psum, g + 1)
                y2 = y[g % 2][:].rearrange("p t d -> p (t d)")
                nc.vector.tensor_tensor(y2, ps[:, 4 + 2 * (g % 2):6 + 2 * (g % 2), :].rearrange("p t d -> p (t d)"), y2, ALU.add).then_inc(summed, 1)

        @block.tensor
        def _(pe):
            pe.wait_ge(wo_in, 16)

            def transposes(g):
                if g >= 2:
                    pe.wait_ge(cT_done, (g - 1) * DT)
                for t in range(DT):
                    for i in range(GT):
                        last = nc.tensor.transpose(ps[:, 2 * (g % 2) + t, i * P:(i + 1) * P], ctx_all[:, g * GT + i, t * P:(t + 1) * P], ident[:])
                    last.then_inc(cT_psum, 1)

            transposes(0)
            for g in range(NGR):
                if g + 1 < NGR:
                    transposes(g + 1)
                pe.wait_ge(cT_done, (g + 1) * DT)
                if g >= 2:
                    pe.wait_ge(summed, g - 1)
                for i in range(GT):
                    for t in range(DT):
                        last = nc.tensor.matmul(ps[:, 4 + 2 * (g % 2) + i // 2, (i % 2) * D:(i % 2 + 1) * D], ctxT[g % 2][:, t, i * P:(i + 1) * P], wo_sb[:, t, :],
                                                start=(t == 0), stop=(t == DT - 1))
                last.then_inc(a_psum, 1)


def program(nc, x, wq, wk, wv_router, wo, bo, w, v, a13, wg, wu, b1, b3, wd, a2, b2, out):
    ctx = ExitStack()
    with ctx:
        q_parts = nc.dram_tensor("q_parts", [H + 1, NP, HD, B * N], BF16, kind="Internal").ap()
        k_parts = nc.dram_tensor("k_parts", [H + 1, NP, HD, B * N], BF16, kind="Internal").ap()
        table = nc.dram_tensor("table", [H + 1, TABLE], F32, kind="Internal").ap()
        y_dram = nc.dram_tensor("y_dram", [B, N, D], F32, kind="Internal").ap()
        v_dram = nc.dram_tensor("v_dram", [B, N, D], F32, kind="Internal").ap()
        ident = ctx.enter_context(nc.sbuf_tensor("ident", [P, P], F32))
        ffn_and_projections(nc, x, wq, wk, wv_router, bo, a13, wg, wu, b1, b3, wd, a2, b2, q_parts, k_parts, v_dram, y_dram, ident)
        v_all = ctx.enter_context(nc.sbuf_tensor("v_all", [P, TT, D], F32))
        attention(nc, q_parts, k_parts, v_dram, table, w, v, v_all, ident)
        output_projection(nc, wo, y_dram, v_all, ident, out)


def kernel(**inputs):
    import numpy as np
    import concourse.bacc as bacc
    from concourse.bass_utils import run_bass_kernel_spmd

    a = {n.replace("L0_", ""): np.asarray(t) for n, t in inputs.items()}
    flat = lambda t: t.transpose(2, 0, 1).reshape(t.shape[2], -1)
    er = lambda t: t.transpose(0, 2, 1).reshape(ER, -1)
    arrays = {
        "x": a["attn_x"], "wq": a["attn_Wq"], "wk": a["attn_Wk"], "wv_router": np.concatenate([a["attn_Wv"], a["ffn_gate_w"].T], axis=1), "wo": a["attn_Wo"], "bo": a["attn_bo"],
        "w": a["attn_w"], "v": a["attn_v"],
        "a13": np.concatenate([flat(a["ffn_A1"]), flat(a["ffn_A3"])], axis=1),
        "wg": a["ffn_w_gate"].T, "wu": a["ffn_w_up"].T, "b1": er(a["ffn_B1"]), "b3": er(a["ffn_B3"]),
        "wd": a["ffn_w_down"].T, "a2": flat(a["ffn_A2"]), "b2": er(a["ffn_B2"]),
    }
    arrays = {n: np.ascontiguousarray(t) for n, t in arrays.items()}
    nc = bacc.Bacc("TRN2", target_bir_lowering=False, num_devices=1)
    args = {n: nc.dram_tensor(n, t.shape, F32, kind="ExternalInput").ap() for n, t in arrays.items()}
    out = nc.dram_tensor("out", [B, N, D], F32, kind="ExternalOutput").ap()
    program(nc, out=out, **args)
    return run_bass_kernel_spmd(nc, [arrays], core_ids=[0]).results[0]["out"]
```
